# Optimizing a Trainium2 kernel written in Bass

```python
import numpy as np
import jax
import jax.numpy as jnp

def _softmax(x, axis=-1):
    return jax.nn.softmax(x, axis=axis)

def _gelu(x):
    return jax.nn.gelu(x, approximate=True)

def _silu(x):
    return jax.nn.silu(x)

def _sigmoid(x):
    return jax.nn.sigmoid(x)

def _layernorm(x, axis=-1, eps=1e-05):
    m = jnp.mean(x, axis=axis, keepdims=True)
    v = jnp.var(x, axis=axis, keepdims=True)
    return (x - m) / jnp.sqrt(v + eps)

def _scatter_add(tgt, idx, src, axis=0):
    return tgt.at[idx].add(src)

def _segment_sum(src, seg, n):
    return jax.ops.segment_sum(src, seg, n)
kernel_name = 'mk_xattn_ffn_d1_seqx_r2_37bf70'

def setup_inputs(seed: int=0):
    np.random.seed(seed)
    _w = jnp.asarray

    def _rec_inputs():
        import jax
        import jax.numpy as jnp
        _rk = jax.random.key(seed)
        x = -7.109e-05 + 0.9999 * jax.random.normal(jax.random.fold_in(_rk, 1), (4, 1024, 1024), jnp.float32)
        _lenS = 1024 - jax.random.randint(jax.random.fold_in(_rk, 7), (4,), 0, max(1, 1024 // 4) + 1, jnp.int32)
        _lenS2 = 1024 - jax.random.randint(jax.random.fold_in(_rk, 8), (4,), 0, max(1, 1024 // 4) + 1, jnp.int32)
        _ctx_2048P = jax.random.normal(jax.random.fold_in(_rk, 11), (4, 16, 1024), jnp.float32)
        _ctx_2048c = jax.random.dirichlet(jax.random.fold_in(_rk, 511), 0.3 * jnp.ones((16,), jnp.float32), (4, 1024))
        _ctx_2048t = jnp.einsum('bsk,bkd->bsd', _ctx_2048c, _ctx_2048P)
        _ctx_2048t = _ctx_2048t * jax.lax.rsqrt(jnp.mean(jnp.square(_ctx_2048t)) + 1e-12) * 0.953939
        ctx_2048 = -3.05549e-07 + 0.0199987 * (_ctx_2048t + 0.3 * jax.random.normal(jax.random.fold_in(_rk, 611), (4, 1024, 1024), jnp.float32))
        return (x, ctx_2048)
    x, ctx_2048 = _rec_inputs()

    def _L0_xattn_setup():
        import jax, jax.numpy as jnp
        import numpy as np
        FP8_MAX = 448.0
        ACT_EPS = 0.0001
        W_EPS = 1e-06
        BLK = 128

        def quant_dequant_act_1x128(x):
            E, M, K = x.shape
            xb = x.reshape(E, M, K // BLK, BLK)
            amax = jnp.max(jnp.abs(xb), axis=-1, keepdims=True)
            safe = jnp.maximum(amax, ACT_EPS)
            q = (xb * (FP8_MAX / safe)).astype(jnp.float8_e4m3fn)
            return (q.astype(jnp.float32) * (safe / FP8_MAX)).reshape(E, M, K)

        def quant_dequant_weight_128x128(w):
            E, N, K = w.shape
            wb = w.reshape(E, N // BLK, BLK, K // BLK, BLK)
            amax = jnp.max(jnp.abs(wb), axis=(2, 4), keepdims=True)
            safe = jnp.maximum(amax, W_EPS)
            q = (wb * (FP8_MAX / safe)).astype(jnp.float8_e4m3fn)
            return (q.astype(jnp.float32) * (safe / FP8_MAX)).reshape(E, N, K)
        key = jax.random.key(seed)
        kx, kw = jax.random.split(key)
        E, M, K, N = (8, 2048, 1024, 1024)
        x = jax.random.normal(kx, (E, M, K), dtype=jnp.float32)
        weight = jax.random.normal(kw, (E, N, K), dtype=jnp.float32) * 0.02
        return {'x': x, 'weight': weight}
    _L0_xattn_all = _L0_xattn_setup()
    _L0_xattn_in = {k: v for k, v in _L0_xattn_all.items() if k in ()}
    del _L0_xattn_all

    def _L0_ffn_setup():
        import jax, jax.numpy as jnp
        import numpy as np
        NUM_EXPERTS = 32
        TOP_K = 6
        N_GROUPS = 4
        N_LIMITED_GROUPS = 2
        key = jax.random.key(seed)
        ks = jax.random.split(key, 8)
        H, M = (1024, 704)
        SH = 2 * M
        s = 0.02
        return {'hidden_states': jax.random.normal(ks[0], (4, 1024, H), jnp.float32), 'gate_w': jax.random.normal(ks[1], (H, NUM_EXPERTS), jnp.float32) * s, 'w_gate': jax.random.normal(ks[2], (NUM_EXPERTS, H, M), jnp.float32) * s, 'w_up': jax.random.normal(ks[3], (NUM_EXPERTS, H, M), jnp.float32) * s, 'w_down': jax.random.normal(ks[4], (NUM_EXPERTS, M, H), jnp.float32) * s, 'sw_gate': jax.random.normal(ks[5], (H, SH), jnp.float32) * s, 'sw_up': jax.random.normal(ks[6], (H, SH), jnp.float32) * s, 'sw_down': jax.random.normal(ks[7], (SH, H), jnp.float32) * s}
    _L0_ffn_all = _L0_ffn_setup()
    _L0_ffn_in = {k: v for k, v in _L0_ffn_all.items() if k in ('gate_w', 'w_gate', 'w_up', 'w_down', 'sw_gate', 'sw_up', 'sw_down')}
    del _L0_ffn_all
    return {'x': x, 'ctx_2048': ctx_2048, 'L0_ffn_gate_w': _L0_ffn_in['gate_w'], 'L0_ffn_w_gate': _L0_ffn_in['w_gate'], 'L0_ffn_w_up': _L0_ffn_in['w_up'], 'L0_ffn_w_down': _L0_ffn_in['w_down'], 'L0_ffn_sw_gate': _L0_ffn_in['sw_gate'], 'L0_ffn_sw_up': _L0_ffn_in['sw_up'], 'L0_ffn_sw_down': _L0_ffn_in['sw_down']}

def reference(x, ctx_2048, L0_ffn_gate_w, L0_ffn_w_gate, L0_ffn_w_up, L0_ffn_w_down, L0_ffn_sw_gate, L0_ffn_sw_up, L0_ffn_sw_down):
    import jax
    import jax.numpy as jnp

    def _L0_xattn_ref(x, weight):
        import jax, jax.numpy as jnp
        import numpy as np
        FP8_MAX = 448.0
        ACT_EPS = 0.0001
        W_EPS = 1e-06
        BLK = 128

        def quant_dequant_act_1x128(x):
            E, M, K = x.shape
            xb = x.reshape(E, M, K // BLK, BLK)
            amax = jnp.max(jnp.abs(xb), axis=-1, keepdims=True)
            safe = jnp.maximum(amax, ACT_EPS)
            q = (xb * (FP8_MAX / safe)).astype(jnp.float8_e4m3fn)
            return (q.astype(jnp.float32) * (safe / FP8_MAX)).reshape(E, M, K)

        def quant_dequant_weight_128x128(w):
            E, N, K = w.shape
            wb = w.reshape(E, N // BLK, BLK, K // BLK, BLK)
            amax = jnp.max(jnp.abs(wb), axis=(2, 4), keepdims=True)
            safe = jnp.maximum(amax, W_EPS)
            q = (wb * (FP8_MAX / safe)).astype(jnp.float8_e4m3fn)
            return (q.astype(jnp.float32) * (safe / FP8_MAX)).reshape(E, N, K)
        xq = quant_dequant_act_1x128(x)
        wq = quant_dequant_weight_128x128(weight)
        return jnp.einsum('emk,enk->emn', xq, wq)

    def _L0_ffn_ref(hidden_states, gate_w, w_gate, w_up, w_down, sw_gate, sw_up, sw_down):
        import jax, jax.numpy as jnp
        import numpy as np
        NUM_EXPERTS = 32
        TOP_K = 6
        N_GROUPS = 4
        N_LIMITED_GROUPS = 2
        B, S, H = hidden_states.shape
        E, K = (NUM_EXPERTS, TOP_K)
        x = hidden_states.reshape(-1, H)
        T = x.shape[0]
        scores = jax.nn.sigmoid(x @ gate_w)
        original_scores = scores
        epg = E // N_GROUPS
        sg = scores.reshape(T, N_GROUPS, epg)
        group_scores = jnp.max(sg, axis=-1)
        _, top_groups = jax.lax.top_k(group_scores, N_LIMITED_GROUPS)
        mask = jnp.ones((T, N_GROUPS), dtype=bool)
        mask = mask.at[jnp.arange(T)[:, None], top_groups].set(False)
        sg = jnp.where(mask[:, :, None], -jnp.inf, sg)
        masked_scores = sg.reshape(T, E)
        _, selected_experts = jax.lax.top_k(masked_scores, K)
        weights = jnp.take_along_axis(original_scores, selected_experts, axis=-1)
        weights = weights / jnp.sum(weights, axis=-1, keepdims=True)
        sel_flat = selected_experts.ravel()
        x_exp = jnp.repeat(x, K, axis=0)
        sort_idx = jnp.argsort(sel_flat)
        xs = x_exp[sort_idx]
        group_sizes = jnp.bincount(sel_flat, length=E).astype(jnp.int32)
        g = jax.lax.ragged_dot(xs, w_gate, group_sizes)
        u = jax.lax.ragged_dot(xs, w_up, group_sizes)
        d = jax.lax.ragged_dot(jax.nn.silu(g) * u, w_down, group_sizes)
        unsort_idx = jnp.argsort(sort_idx)
        out = d[unsort_idx].reshape(T, K, H)
        expert_out = jnp.sum(out * weights[..., None], axis=1)
        shared = jax.nn.silu(x @ sw_gate) * (x @ sw_up) @ sw_down
        return (expert_out + shared).reshape(B, S, H)
    x = x + _L0_xattn_ref(_layernorm(x, axis=-1), ctx_2048)
    x = x + _L0_ffn_ref(_layernorm(x, axis=-1), L0_ffn_gate_w, L0_ffn_w_gate, L0_ffn_w_up, L0_ffn_w_down, L0_ffn_sw_gate, L0_ffn_sw_up, L0_ffn_sw_down)
    return x

_drawn_inputs = setup_inputs


def setup_inputs(seed=0):
    import zlib

    import numpy as np

    out = dict(_drawn_inputs(seed))
    spreads = {}
    factors = {}
    for name, (base, spread) in spreads.items():
        noise = np.random.default_rng([zlib.crc32(name.encode()), seed]).standard_normal(out[name].shape)
        drawn = base * np.exp(spread * noise) if base else spread * noise
        out[name] = jnp.asarray(drawn.astype(out[name].dtype))
    for name, factor in factors.items():
        out[name] = (out[name] * factor).astype(out[name].dtype)
    return out
```

```python
from contextlib import ExitStack

import concourse.bass as bass
from concourse import mybir

F32 = mybir.dt.float32
F16 = mybir.dt.float16
I32 = mybir.dt.int32
U32 = mybir.dt.uint32
ALU = mybir.AluOpType
ACT = mybir.ActivationFunctionType
AX = mybir.AxisListType
ds = bass.ds

P = 128
B, S, H = 4, 1024, 1024
E, TOPK, GROUPS, TOPG = 32, 6, 4, 2
M = 704
KH = H // P
KM = -(-M // P)
M_LAST = M - (KM - 1) * P
T = B * S
TT = T // P
BT = S // P
CH = M // 2
FULL = T * TOPK // P
EXTRA = E - 1
SLOT_TILES = FULL + EXTRA
GU = KH * 2 * M
WCOLS = GU + KM * H
CHUNKS = KH + KM
STAGES = 4

FP8_MAX, ACT_EPS, W_EPS, LN_EPS = 448.0, 1e-4, 1e-6, 1e-5
EXP_MASK = 0x7F800000
FP8_MIN_EXP = 2.0 ** -6
FP8_ROUND = 1.5 * 2.0 ** 20
WSCALE = 256.0
HSCALE = 16.0
FAR = 2.0 ** 20
NEG = -1.0e30



class Chain:

    def __init__(self, engine, sem, base):
        self.engine, self.sem, self.base, self.n = engine, sem, base, 0

    def __call__(self, instruction):
        self.n += 1
        instruction.then_inc(self.sem, 1)
        self.engine.wait_ge(self.sem, self.base + self.n)


def build(nc, x, ctx_in, gate_w, w_gate, w_up, w_down, sw_gate, sw_up, sw_down, out):
    x_rows = x.rearrange("b s d -> (b s) d")
    c_rows = ctx_in.rearrange("b s d -> (b s) d")
    o_rows = out.rearrange("b s d -> (b s) d")

    rows_x = nc.dram_tensor("rows_x", (T + SLOT_TILES * P, 2 * H), F16).ap()
    rows_d = nc.dram_tensor("rows_d", (T + SLOT_TILES * P, H), F32).ap()
    rows_x1 = nc.dram_tensor("rows_x1", (T, H), F32).ap()
    last_row = T + SLOT_TILES * P - 1

    with ExitStack() as stack:
        def sb(name, shape, dt):
            return stack.enter_context(nc.sbuf_tensor(name, shape, dt))

        def psum(name, shape, dt):
            return stack.enter_context(nc.psum_tensor(name, shape, dt))

        def sem(name):
            return stack.enter_context(nc.semaphore(name))

        wts = sb("wts", [P, 2, 2, WCOLS], F16)
        stage = sb("stage", [P, STAGES, 2 * M], F32)
        xin = sb("xin", [P, 2, H], F16)
        xT = sb("xT", [P, 2, KH, P], F16)
        sil = sb("sil", [P, 2, CH], F32)
        hid = sb("hid", [P, 2, CH], F32)
        hid_hl = sb("hid_hl", [P, 2, M], F16)
        hT = sb("hT", [P, 2, H], F16)
        dout = sb("dout", [P, H], F32)
        ident = sb("ident", [P, P], F16)
        upper = sb("upper", [P, P], F16)
        ones = sb("ones", [P, P], F16)
        ones_f = sb("ones_f", [P, E], F32)
        gw_f = sb("gw_f", [P, KH * E], F32)
        gw = sb("gw", [P, 2, KH * E], F16)
        iota_e = sb("iota_e", [P, E], F32)
        iota_p = sb("iota_p", [P, 1], F32)
        iota_t = sb("iota_t", [P, SLOT_TILES], F32)
        amax_p, amax, safe, to_q, from_q = (sb(n, [P, KH], F32) for n in ("amax_p", "amax", "safe", "to_q", "from_q"))
        stats_q, stats_l = sb("stats_q", [P, 12], F32), sb("stats_l", [P, 12], F32)
        mv_q, mv_l = sb("mv_q", [P, 2], F32), sb("mv_l", [P, 2], F32)
        var_q, var_l = sb("var_q", [P, 1], F32), sb("var_l", [P, 1], F32)
        std_q, std_l = sb("std_q", [P, 1], F32), sb("std_l", [P, 1], F32)
        rstd_q, rstd_l = sb("rstd_q", [P, 1], F32), sb("rstd_l", [P, 1], F32)
        group8, group_top, expert_top = (sb(n, [P, 8], F32) for n in ("group8", "group_top", "expert_top"))
        group_idx, expert_idx = sb("group_idx", [P, 8], U32), sb("expert_idx", [P, 8], U32)
        group_f = sb("group_f", [P, TOPG], F32)
        chosen, chosen2 = sb("chosen", [P, GROUPS], F32), sb("chosen2", [P, GROUPS], F32)
        masked = sb("masked", [P, E], F32)
        top_idx = sb("top_idx", [P, TT, TOPK], F32)
        top_w = sb("top_w", [P, TT, TOPK], F32)
        w_sum = sb("w_sum", [P, TT], F32)
        slot = sb("slot", [P, TT, TOPK], I32)
        count = sb("count", [P, E], F32)
        tiles_e, ends, first_slot, tmp_e = (sb(n, [P, E], F32) for n in ("tiles_e", "ends", "first_slot", "tmp_e"))
        expert_t = sb("expert_t", [1, SLOT_TILES], F32)
        ready_tab = sb("ready_tab", [1, TT + SLOT_TILES], I32)
        buf_tab = sb("buf_tab", [1, TT + SLOT_TILES], I32)
        done_tab = sb("done_tab", [1, E + 2], I32)
        count_tab = sb("count_tab", [1, 1], I32)
        pad_idx = sb("pad_idx", [P, E], I32)
        pad_now = sb("pad_now", [P, 4], I32)
        slot_now = sb("slot_now", [P, 2, TOPK], I32)

        early = wts[:, 1, :, :].rearrange("p a c -> p (a c)")
        cT = early[:, 0:2 * KH * S].rearrange("p (a k n) -> p a k n", a=2, k=KH)
        xqT = xin[:, :, :].rearrange("p a (k n) -> p a k n", k=KH)
        e0 = 2 * KH * S
        qin, xres, x1b, t0, t1, t2 = (early[:, e0 + 2 * H * i:e0 + 2 * H * (i + 1)].bitcast(F32) for i in range(6))
        nat = early[:, e0 + 2 * H * 6:e0 + 2 * H * 7].rearrange("p (a d) -> p a d", a=2)
        x2nat = early[:, e0 + 2 * H * 7:e0 + 2 * H * 8].rearrange("p (a d) -> p a d", a=2)
        n_hot = 2 * TT * TOPK * E
        hot, prod = (early[:, i * n_hot:(i + 1) * n_hot].bitcast(F32).rearrange("p (t k e) -> p t k e", t=TT, k=TOPK)
                     for i in range(2))
        mask, pre_a, pre_b = (early[:, 2 * n_hot + TT * E * i:2 * n_hot + TT * E * (i + 1)]
                              .rearrange("p (t e) -> p t e", t=TT) for i in range(3))
        place = early[:, 2 * n_hot + TT * E * 3:2 * n_hot + TT * E * 5].bitcast(F32).rearrange("p (t e) -> p t e", t=TT)
        tab_cmp = early[0:1, 0:2 * SLOT_TILES * E].bitcast(F32).rearrange("p (t e) -> p t e", t=SLOT_TILES)
        xsc = [early[:, 2 * H * i:2 * H * (i + 1)] for i in range(2)]
        zeros = early[:, 4 * H:6 * H]
        late = wts[:, 0, :, :].rearrange("p a c -> p (a c)").bitcast(F32)
        gat = [late[:, u * TOPK * H:(u + 1) * TOPK * H].rearrange("p (k d) -> p k d", k=TOPK) for u in range(2)]
        total = [late[:, (2 * TOPK + u) * H:(2 * TOPK + u + 1) * H] for u in range(2)]
        a_rows = [late[:, (2 * TOPK + 2 + u) * H:(2 * TOPK + 3 + u) * H] for u in range(2)]

        ps_t = psum("ps_t", [P, 2, H], F16)
        ps_gu = psum("ps_gu", [P, 4, 512], F32)
        ps_d = psum("ps_d", [P, 2, 512], F32)
        ps_d_flat = ps_d[:, :, :].rearrange("p a n -> p (a n)")
        ps_logits = ps_gu[:, 0, 0:E]

        const_ready, pool_step, gw_in, gw_step, gw_ready = (sem(n) for n in (
            "const_ready", "pool_step", "gw_in", "gw_step", "gw_ready"))
        conv_step, conv_done, weights_ready = (sem(n) for n in ("conv_step", "conv_done", "weights_ready"))
        qin_in, qin_free, xres_in, block_max, block_max_all, var_ready, std_ready = (sem(n) for n in (
            "qin_in", "qin_free", "xres_in", "block_max", "block_max_all", "var_ready", "std_ready"))
        nat_ready, nat_free, x1_free, x2_ready, x2_free = (sem(n) for n in (
            "nat_ready", "nat_free", "x1_free", "x2_ready", "x2_free"))
        tr_done, tr_free, attn_done, logits_done, logits_free, x1_out, x2_out, sp_turn = (sem(n) for n in (
            "tr_done", "tr_free", "attn_done", "logits_done", "logits_free", "x1_out", "x2_out", "sp_turn"))
        ctx_step, x_step, ln_step, top_step = (sem(n) for n in ("ctx_step", "x_step", "ln_step", "top_step"))
        route_step, top_ready, sig_ready, mask_ready, rank_done, routed, pad_out = (sem(n) for n in (
            "route_step", "top_ready", "sig_ready", "mask_ready", "rank_done", "routed", "pad_out"))
        xin_in, trx, xt_high, xt_low, gu_done, silu_done = (sem(n) for n in (
            "xin_in", "trx", "xt_high", "xt_low", "gu_done", "silu_done"))
        hid_done, hid_high, hid_low, trh, ht_high, ht_low, down_done, d_free, d_out = (sem(n) for n in (
            "hid_done", "hid_high", "hid_low", "trh", "ht_high", "ht_low", "down_done", "d_free", "d_out"))
        pe_turn, dve_turn, pool_turn = (sem(n) for n in ("pe_turn", "dve_turn", "pool_turn"))
        comb_step, comb_done, o_out = (sem(n) for n in ("comb_step", "comb_done", "o_out"))
        stage_in = [sem(f"stage_in{i}") for i in range(STAGES)]
        xsc_in = [sem(f"xsc_in{u}") for u in range(2)]
        scat_out = [sem(f"scat_out{u}") for u in range(2)]
        gat_in = [sem(f"gat_in{u}") for u in range(2)]
        side_in = [sem(f"side_in{u}") for u in range(2)]

        CONSTS = 9
        SETS = 3 * BT
        N_ALL = TT + FULL
        N_B = TT + SLOT_TILES
        A_LAST = TT - 2
        CTX_STEPS, X_STEPS, LN_STEPS, TOP_STEPS, COMB_STEPS = 9, 14, 5, 10, 6

        def stage_of(o, c):
            return (o * CHUNKS + c) % STAGES

        def loads_of(o, c):
            return sum((g % STAGES) == stage_of(o, c) for g in range(o * CHUNKS + c + 1))

        pair_loads = [sum(g % STAGES == st for g in range(2 * CHUNKS)) for st in range(STAGES)]

        block = stack.enter_context(nc.Block())

        @block.sync
        def _(sp):
            def load_piece(o, c, gate, up, down):
                st = stage_of(o, c)
                if c < KH:
                    sp.dma_start(stage[:, st, 0:M], gate[c * P:(c + 1) * P, :]).then_inc(stage_in[st], 16)
                    sp.dma_start(stage[:, st, M:2 * M], up[c * P:(c + 1) * P, :]).then_inc(stage_in[st], 16)
                else:
                    r0 = (c - KH) * P
                    n = min(P, M - r0)
                    for h in range(2):
                        sp.dma_start(stage[0:n, st, h * 512:(h + 1) * 512],
                                     down[r0:r0 + n, h * 512:(h + 1) * 512]).then_inc(stage_in[st], 16)

            half_a = (sw_gate[:, 0:M], sw_up[:, 0:M], sw_down[0:M, :])
            half_b = (sw_gate[:, M:2 * M], sw_up[:, M:2 * M], sw_down[M:2 * M, :])
            sp.dma_start(gw_f[:, :].rearrange("p (k e) -> p k e", k=KH),
                         gate_w.rearrange("(k p) e -> p k e", p=P)).then_inc(gw_in, 16)
            for c in range(STAGES):
                load_piece(0, c, *half_a)

            def load_q(rows, row, n):
                sp.wait_ge(qin_free, n + 1)
                sp.dma_start(qin, rows[ds(row, P), :]).then_inc(qin_in, 16)

            def load_res(i):
                sp.dma_start(xres, x_rows[ds(i * P, P), :]).then_inc(xres_in, 16)

            def store_tile(i):
                sp.wait_ge(x1_free, i + 2)
                sp.dma_start(rows_x1[ds(i * P, P), :], x1b).then_inc(x1_out, 16)
                sp.wait_ge(x2_ready, i + 1)
                sp.dma_start(rows_x[ds(i * P, P), :], x2nat.rearrange("p a d -> p (a d)")).then_inc(x2_out, 16)
                sp.wait_ge(x1_out, i * 16 + 16)
                sp.wait_ge(x2_out, i * 16 + 16)

            with sp.Fori(0, B) as b:
                with sp.Fori(0, BT) as j:
                    load_q(c_rows, (b * BT + j) * P, b * (2 * BT) + j)
                load_q(x_rows, b * (BT * P), b * (2 * BT) + BT)
                load_res(b * BT)
                with sp.Fori(0, BT - 1) as j:
                    load_q(x_rows, (b * BT + j + 1) * P, b * (2 * BT) + j + BT + 1)
                    store_tile(b * BT + j)
                    load_res(b * BT + j + 1)
                store_tile(b * BT + (BT - 1))
                sp.sem_inc(sp_turn, 1)

            for c in range(STAGES, CHUNKS):
                sp.wait_ge(conv_done, c - STAGES + 1)
                load_piece(0, c, *half_a)

            sp.wait_ge(routed, 1)
            for u in range(2):
                sp.dma_start(xsc[u], rows_x[u * P:(u + 1) * P, :]).then_inc(xsc_in[u], 16)
            with sp.Fori(1, TT // 2) as q:
                for u in range(2):
                    sp.wait_ge(scat_out[u], q * (16 * TOPK))
                    sp.dma_start(xsc[u], rows_x[ds((q * 2 + u) * P, P), :]).then_inc(xsc_in[u], 16)

            with sp.Fori(0, E // 2) as q:
                for u in range(2):
                    mats = [w[ds(q * 2 + u, 1)].rearrange("a r c -> (a r) c") for w in (w_gate, w_up, w_down)]
                    for c in range(CHUNKS):
                        sp.wait_ge(conv_done, q * (2 * CHUNKS) + ((1 + u) * CHUNKS + c - STAGES + 1))
                        load_piece(1 + u, c, *mats)
            for c in range(CHUNKS):
                sp.wait_ge(conv_done, (E + 1) * CHUNKS + c - STAGES + 1)
                load_piece(1, c, *half_b)

            sp.wait_ge(down_done, N_B)
            sp.wait_ge(d_out, 16 * N_B)

            def side(i, u):
                sp.dma_start(total[u], rows_x1[ds(i * P, P), :]).then_inc(side_in[u], 16)
                sp.dma_start(a_rows[u], rows_d[ds(i * P, P), :]).then_inc(side_in[u], 16)

            def store_out(i, u):
                sp.wait_ge(comb_done, i + 1)
                sp.dma_start(o_rows[ds(i * P, P), :], total[u]).then_inc(o_out, 16)

            side(0, 0)
            side(1, 1)
            with sp.Fori(0, TT // 2 - 1) as q:
                for u in range(2):
                    store_out(q * 2 + u, u)
                    sp.wait_ge(o_out, q * 32 + 16 * (u + 1))
                    side(q * 2 + u + 2, u)
            store_out(TT - 2, 0)
            store_out(TT - 1, 1)
            sp.wait_ge(o_out, 16 * TT)

        @block.gpsimd
        def _(pool):
            g = nc.gpsimd
            g.memset(ident[:, :], 0.0).then_inc(pool_step, 1)
            g.memset(upper[:, :], 1.0).then_inc(pool_step, 1)
            g.memset(ones[:, :], 1.0).then_inc(const_ready, 1)
            g.memset(ones_f[:, :], 1.0).then_inc(const_ready, 1)
            g.memset(group8[:, :], -3.0e38).then_inc(const_ready, 1)
            pool.wait_ge(pool_step, 2)
            g.affine_select(out=ident[:, :], in_=ident[:, :], compare_op=ALU.not_equal, fill=1.0, base=0,
                            pattern=[[-1, P]], channel_multiplier=1).then_inc(const_ready, 1)
            g.affine_select(out=upper[:, :], in_=upper[:, :], compare_op=ALU.is_gt, fill=0.0, base=0,
                            pattern=[[1, P]], channel_multiplier=-1).then_inc(const_ready, 1)
            g.iota(iota_e[:, :], pattern=[[1, E]], base=0, channel_multiplier=0,
                   allow_small_or_imprecise_dtypes=True).then_inc(const_ready, 1)
            g.iota(iota_p[:, :], pattern=[[0, 1]], base=0, channel_multiplier=1,
                   allow_small_or_imprecise_dtypes=True).then_inc(const_ready, 1)
            g.iota(iota_t[:, :], pattern=[[1, SLOT_TILES]], base=0, channel_multiplier=0,
                   allow_small_or_imprecise_dtypes=True).then_inc(const_ready, 1)
            g.memset(amax[:, :], 0.0).then_inc(const_ready, 1)

            def split_piece(o, c, buf, pair=0):
                st = stage_of(o, c)
                n, cols, at = (P, 2 * M, c * 2 * M) if c < KH else \
                    (min(P, M - (c - KH) * P), H, GU + (c - KH) * H)
                high, low = wts[0:n, buf, 0, at:at + cols], wts[0:n, buf, 1, at:at + cols]
                raw = stage[0:n, st, 0:cols]
                step = pair * (4 * CHUNKS) + 2 * (o * CHUNKS + c)
                pool.wait_ge(stage_in[st], pair * (32 * pair_loads[st]) + 32 * loads_of(o, c))
                pool.sem_inc(pool_turn, 1)
                g.tensor_scalar(high, raw, WSCALE, 1.0, ALU.mult, ALU.mult).then_inc(conv_step, 1)
                g.tensor_scalar(raw, raw, WSCALE, 1.0, ALU.mult, ALU.mult).then_inc(conv_step, 1)
                pool.wait_ge(conv_step, step + 2)
                g.tensor_tensor(low, raw, high, ALU.subtract).then_inc(conv_done, 1)

            for c in range(STAGES):
                split_piece(0, c, 0)
            with pool.Fori(0, B * BT) as c:
                pool.wait_ge(block_max, c + 1)
                pool.sem_inc(pool_turn, 1)
                g.partition_all_reduce(amax[:, :], amax_p[:, :], P,
                                       bass.bass_isa.ReduceOp.max).then_inc(block_max_all, 1)
            for c in range(STAGES, CHUNKS):
                split_piece(0, c, 0)
            pool.wait_ge(conv_done, CHUNKS)
            pool.sem_inc(weights_ready, 1)

            pool.wait_ge(routed, 1)
            g.memset(zeros, 0.0).then_inc(pool_step, 1)
            pool.wait_ge(pool_step, 3)

            def pad_four(q):
                g.tensor_copy(pad_now[:, :], pad_idx[:, ds(q * 4, 4)]).then_inc(pool_step, 1)
                pool.wait_ge(pool_step, q + 4)
                pool.sem_inc(pool_turn, 1)
                for u in range(4):
                    g.indirect_dma_start(
                        out=rows_x, out_offset=bass.IndirectOffsetOnAxis(ap=pad_now[:, u:u + 1], axis=0),
                        in_=zeros, in_offset=None, bounds_check=last_row, oob_is_err=False).then_inc(pad_out, 16)

            pad_four(0)
            with pool.Fori(1, E // 4) as q:
                pool.wait_ge(pad_out, q * 64)
                pad_four(q)

            with pool.Fori(0, TT // 2) as q:
                for u in range(2):
                    pool.wait_ge(xsc_in[u], q * 16 + 16)
                    g.tensor_copy(slot_now[:, u, :], slot[:, ds(q * 2 + u, 1), :].rearrange("p a k -> p (a k)")
                                  ).then_inc(pool_step, 1)
                    pool.wait_ge(pool_step, q * 2 + (u + 4 + E // 4))
                    pool.sem_inc(pool_turn, 1)
                    for k in range(TOPK):
                        g.indirect_dma_start(
                            out=rows_x, out_offset=bass.IndirectOffsetOnAxis(ap=slot_now[:, u, k:k + 1], axis=0),
                            in_=xsc[u], in_offset=None, bounds_check=last_row,
                            oob_is_err=False).then_inc(scat_out[u], 16)
            pool.wait_ge(pad_out, 16 * E)
            for u in range(2):
                pool.wait_ge(scat_out[u], 16 * TOPK * TT // 2)

            with pool.Fori(0, E // 2) as q:
                for u in range(2):
                    done = pool.value_load(done_tab[0:1, ds(q * 2 + u, 1)], min_val=1, max_val=N_B)
                    pool.wait_ge(down_done, done)
                    pool.sem_inc(pool_turn, 1)
                    for c in range(CHUNKS):
                        split_piece(1 + u, c, 1 - u, q)
                    pool.wait_ge(conv_done, q * (2 * CHUNKS) + (2 + u) * CHUNKS)
                    pool.sem_inc(weights_ready, 1)
            done = pool.value_load(done_tab[0:1, E:E + 1], min_val=1, max_val=N_B)
            pool.wait_ge(down_done, done)
            pool.sem_inc(pool_turn, 1)
            for c in range(CHUNKS):
                split_piece(1, c, 1, E // 2)
            pool.wait_ge(conv_done, (E + 2) * CHUNKS)
            pool.sem_inc(weights_ready, 1)

            pool.wait_ge(down_done, N_B)
            pool.wait_ge(d_out, 16 * N_B)

            def gather(i, u, step):
                g.tensor_copy(slot_now[:, u, :], slot[:, ds(i, 1), :].rearrange("p a k -> p (a k)")
                              ).then_inc(pool_step, 1)
                pool.wait_ge(pool_step, step)
                pool.sem_inc(pool_turn, 1)
                for k in range(TOPK):
                    g.indirect_dma_start(
                        out=gat[u][:, k, :], out_offset=None, in_=rows_d,
                        in_offset=bass.IndirectOffsetOnAxis(ap=slot_now[:, u, k:k + 1], axis=0),
                        bounds_check=last_row, oob_is_err=False).then_inc(gat_in[u], 16)

            step0 = 3 + E // 4 + TT
            gather(0, 0, step0 + 1)
            gather(1, 1, step0 + 2)
            with pool.Fori(1, TT // 2) as q:
                for u in range(2):
                    pool.wait_ge(comb_done, q * 2 + (u - 1))
                    gather(q * 2 + u, u, q * 2 + (u + 1 + step0))

        @block.tensor
        def _(pe):
            def transposes(src, blocks, width_last=P):
                for a in range(2):
                    for k in range(blocks):
                        w = width_last if k == blocks - 1 else P
                        last = nc.tensor.transpose(ps_t[0:w, a, k * P:(k + 1) * P], src[:, a, k * P:k * P + w],
                                                   ident[:, :])
                return last

            def three(dst, high, low, w_high, w_low, first, last):
                n = len(dst)
                for a, (left, right) in enumerate(((high, w_high), (high, w_low), (low, w_high))):
                    for c in range(n):
                        ins = nc.tensor.matmul(dst[c], left, right[c], start=(first and a == 0),
                                               stop=(last and a == 2))
                return ins

            pe.wait_ge(const_ready, CONSTS)
            pe.wait_ge(gw_ready, 1)

            def tr(src, t, ready, n):
                pe.wait_ge(ready, n)
                pe.wait_ge(tr_free, t + 1)
                transposes(src, KH).then_inc(tr_done, 1)

            def attend(i, t):
                pe.wait_ge(tr_free, t + 2)
                pe.wait_ge(x1_free, i + 1)
                for k in range(KH):
                    ins = three([ps_d[:, c, :] for c in range(2)], xqT[:, 0, k, :], xqT[:, 1, k, :],
                                [cT[:, 0, k, c * 512:(c + 1) * 512] for c in range(2)],
                                [cT[:, 1, k, c * 512:(c + 1) * 512] for c in range(2)], k == 0, k == KH - 1)
                ins.then_inc(attn_done, 1)

            def logits(i, t):
                pe.wait_ge(tr_free, t + 2)
                pe.wait_ge(logits_free, i + 1)
                for k in range(KH):
                    ins = three([ps_logits], xT[:, 0, k, :], xT[:, 1, k, :], [gw[:, 0, k * E:(k + 1) * E]],
                                [gw[:, 1, k * E:(k + 1) * E]], k == 0, k == KH - 1)
                ins.then_inc(logits_done, 1)

            with pe.Fori(0, B) as b:
                with pe.Fori(0, BT) as j:
                    tr(nat, b * SETS + j, nat_ready, b * (2 * BT) + j + 1)
                tr(nat, b * SETS + BT, nat_ready, b * (2 * BT) + (BT + 1))
                attend(b * BT, b * SETS + BT)
                with pe.Fori(1, BT) as j:
                    tr(nat, b * SETS + j * 2 + (BT - 1), nat_ready, b * (2 * BT) + j + (BT + 1))
                    attend(b * BT + j, b * SETS + j * 2 + (BT - 1))
                    tr(x2nat, b * SETS + j * 2 + BT, x2_ready, b * BT + j)
                    logits(b * BT + j - 1, b * SETS + j * 2 + BT)
                tr(x2nat, b * SETS + (SETS - 1), x2_ready, b * BT + BT)
                logits(b * BT + (BT - 1), b * SETS + (SETS - 1))

            pe.wait_ge(mask_ready, 1)
            half = TT // 2
            for c in range(2):
                nc.tensor.matmul(ps_gu[:, c, :], upper[:, :],
                                 mask[:, c * half:(c + 1) * half, :].rearrange("p t e -> p (t e)"),
                                 start=True, stop=False)
                nc.tensor.matmul(ps_gu[:, c, :], ones[:, :],
                                 pre_b[:, c * half:(c + 1) * half, :].rearrange("p t e -> p (t e)"),
                                 start=False, stop=True)
            nc.tensor.matmul(ps_gu[:, 2, 0:E], ones[:, :], mask[:, TT - 1, :], start=True, stop=False)
            nc.tensor.matmul(ps_gu[:, 2, 0:E], ones[:, :], pre_b[:, TT - 1, :], start=False,
                             stop=True).then_inc(rank_done, 1)
            pe.wait_ge(routed, 1)

            def tr_x(n):
                pe.wait_ge(xin_in, n * 16 + 16)
                transposes(xin, KH).then_inc(trx, 1)

            def gate_up(n, buf):
                for k in range(KH):
                    cols = [k * 2 * M + c * CH for c in range(4)]
                    ins = three([ps_gu[:, c, 0:CH] for c in range(4)], xT[:, 0, k, :], xT[:, 1, k, :],
                                [wts[:, buf, 0, a:a + CH] for a in cols],
                                [wts[:, buf, 1, a:a + CH] for a in cols], k == 0, k == KH - 1)
                ins.then_inc(gu_done, 1)

            def tr_h(n):
                pe.wait_ge(hid_high, n + 1)
                pe.wait_ge(hid_low, n + 1)
                transposes(hid_hl, KM, M_LAST).then_inc(trh, 1)

            def down(n, buf):
                for k in range(KM):
                    r = P if k < KM - 1 else M_LAST
                    cols = [GU + k * H + c * 512 for c in range(2)]
                    ins = three([ps_d[:, c, :] for c in range(2)], hT[0:r, 0, k * P:(k + 1) * P],
                                hT[0:r, 1, k * P:(k + 1) * P],
                                [wts[0:r, buf, 0, a:a + 512] for a in cols],
                                [wts[0:r, buf, 1, a:a + 512] for a in cols], k == 0, k == KM - 1)
                ins.then_inc(down_done, 1)

            def buffer_of(n):
                return pe.value_load(buf_tab[0:1, ds(n, 1)], min_val=0, max_val=1)

            def by_buffer(product, n, which):
                if isinstance(which, int):
                    product(n, which)
                    return
                with pe.If(which < 1):
                    product(n, 0)
                with pe.Else():
                    product(n, 1)

            def weights_of(n, ready):
                if ready is None:
                    ready = pe.value_load(ready_tab[0:1, ds(n, 1)], min_val=1, max_val=E + 1)
                pe.wait_ge(weights_ready, ready)

            def tile(n, buf=None, ready=None, first=False, last=False, buf_before=None):
                if buf is None:
                    buf = buffer_of(n)
                if buf_before is None and not first:
                    buf_before = buffer_of(n - 1)
                weights_of(n, ready)
                pe.wait_ge(xt_high, n + 1)
                pe.wait_ge(xt_low, n + 1)
                if not first:
                    pe.wait_ge(hid_done, n)
                by_buffer(gate_up, n, buf)
                if not first:
                    pe.wait_ge(ht_high, n)
                    pe.wait_ge(ht_low, n)
                if not last:
                    tr_x(n + 1)
                if not first:
                    pe.wait_ge(d_free, n)
                    by_buffer(down, n - 1, buf_before)
                if not last:
                    pe.wait_ge(xt_high, n + 2)
                    pe.wait_ge(xt_low, n + 2)
                tr_h(n)

            def drain_tile(n, buf=None):
                if buf is None:
                    buf = buffer_of(n)
                pe.wait_ge(ht_high, n + 1)
                pe.wait_ge(ht_low, n + 1)
                pe.wait_ge(d_free, n + 1)
                by_buffer(down, n, buf)

            pe.wait_ge(tr_free, B * SETS + 1)
            tr_x(0)
            tile(0, 0, 1, first=True)
            with pe.Fori(1, N_ALL - 1) as n:
                tile(n)
            tile(N_ALL - 1, last=True)
            drain_tile(N_ALL - 1)

            n_tiles = pe.value_load(count_tab[0:1, 0:1], min_val=N_ALL, max_val=N_B)
            with pe.Fori(N_ALL, N_B) as n:
                with pe.If(n < n_tiles):
                    tr_x(n)
                    buf = buffer_of(n)
                    weights_of(n, None)
                    pe.wait_ge(xt_high, n + 1)
                    pe.wait_ge(xt_low, n + 1)
                    by_buffer(gate_up, n, buf)
                    tr_h(n)
                    drain_tile(n, buf)
                with pe.Else():
                    pe.wait_ge(down_done, n)
                    for done in (trx, gu_done, trh, down_done):
                        pe.sem_inc(done, 1)

            tr_x(N_B)
            tile(N_B, 1, E + 2, first=True)
            with pe.Fori(N_B + 1, N_B + TT - 1) as n:
                tile(n, 1, E + 2, buf_before=1)
            tile(N_B + TT - 1, 1, E + 2, last=True, buf_before=1)
            drain_tile(N_B + TT - 1, 1)

        @block.scalar
        def _(act):
            a = nc.scalar
            act.sem_inc(tr_free, 1)
            act.sem_inc(nat_free, 1)
            act.sem_inc(x2_free, 1)
            act.sem_inc(d_free, 1)

            def take(high, low, t, rows_free):
                act.wait_ge(tr_done, t + 1)
                act.sem_inc(rows_free, 1)
                a.activation(high, ps_t[:, 0, :].rearrange("p (k n) -> p k n", k=KH), ACT.Copy)
                a.activation(low, ps_t[:, 1, :].rearrange("p (k n) -> p k n", k=KH), ACT.Copy).then_inc(tr_free, 1)

            def take_q(t):
                take(xqT[:, 0], xqT[:, 1], t, nat_free)

            def take_x2(t):
                take(xT[:, 0], xT[:, 1], t, x2_free)

            def root(std, var, n):
                act.wait_ge(var_ready, n + 1)
                a.activation(std[:, :], var[:, :], ACT.Sqrt).then_inc(std_ready, 1)

            with act.Fori(0, B) as b:
                with act.Fori(0, BT) as j:
                    cols = [cT[:, h, :, ds(j * P, P)] for h in range(2)]
                    take(cols[0], cols[1], b * SETS + j, nat_free)
                root(std_q, var_q, b * (2 * BT))
                take_q(b * SETS + BT)
                root(std_q, var_q, b * (2 * BT) + 1)
                root(std_l, var_l, b * (2 * BT) + 2)
                with act.Fori(1, BT - 1) as j:
                    take_q(b * SETS + j * 2 + (BT - 1))
                    root(std_q, var_q, b * (2 * BT) + j * 2 + 1)
                    take_x2(b * SETS + j * 2 + BT)
                    root(std_l, var_l, b * (2 * BT) + j * 2 + 2)
                take_q(b * SETS + (SETS - 3))
                take_x2(b * SETS + (SETS - 2))
                root(std_l, var_l, b * (2 * BT) + (2 * BT - 1))
                take_x2(b * SETS + (SETS - 1))

            act.wait_ge(top_ready, 1)
            a.activation(top_w[:, :, :], top_w[:, :, :], ACT.Sigmoid, scale=1.0 / WSCALE).then_inc(sig_ready, 1)

            def load_x(n, row):
                act.dma_start(xin[:, :, :].rearrange("p a d -> p (a d)"), rows_x[ds(row, P), :]).then_inc(xin_in, 16)

            def take_xt(n):
                act.wait_ge(trx, n + 1)
                a.activation(xT[:, 0, :, :], ps_t[:, 0, :].rearrange("p (k n) -> p k n", k=KH), ACT.Copy)\
                    .then_inc(xt_high, 1)

            def silu(n):
                act.wait_ge(gu_done, n + 1)
                a.activation(sil[:, :, :], ps_gu[:, 0:2, 0:CH], ACT.Silu, scale=1.0 / WSCALE).then_inc(silu_done, 1)

            def high_of_hidden(n):
                act.wait_ge(hid_done, n + 1)
                a.activation(hid_hl[:, 0, :], hid[:, :, :].rearrange("p a c -> p (a c)"), ACT.Copy)\
                    .then_inc(hid_high, 1)

            def take_ht(n):
                act.wait_ge(trh, n + 1)
                a.activation(hT[:, 0, 0:KM * P], ps_t[:, 0, 0:KM * P], ACT.Copy).then_inc(ht_high, 1)

            def store_d(n, free=True):
                act.wait_ge(down_done, n + 1)
                if free:
                    act.wait_ge(d_out, n * 16)
                a.activation(dout[:, :], ps_d_flat, ACT.Copy, scale=1.0 / (WSCALE * HSCALE)).then_inc(d_free, 1)
                act.wait_ge(d_free, n + 2)
                act.dma_start(rows_d[ds(n * P, P), :], dout[:, :]).then_inc(d_out, 16)

            def tile(n, next_row=None, last=False, before="none"):
                silu(n)
                if not last:
                    take_xt(n + 1)
                if next_row is not None:
                    load_x(n + 2, next_row)
                high_of_hidden(n)
                if before != "none":
                    store_d(n - 1, before == "free")
                take_ht(n)

            act.wait_ge(x2_out, 16 * TT)
            act.wait_ge(routed, 1)
            load_x(0, 0)
            take_xt(0)
            load_x(1, P)
            tile(0, 2 * P)
            tile(1, 3 * P, before="fresh")
            with act.Fori(2, A_LAST) as n:
                tile(n, (n + 2) * P, before="free")
            act.wait_ge(pad_out, 16 * E)
            for u in range(2):
                act.wait_ge(scat_out[u], 16 * TOPK * TT // 2)
            with act.Fori(A_LAST, N_ALL - 2) as n:
                tile(n, (n + 2) * P, before="free")
            tile(N_ALL - 2, before="free")
            tile(N_ALL - 1, last=True, before="free")
            store_d(N_ALL - 1)

            n_tiles = act.value_load(count_tab[0:1, 0:1], min_val=N_ALL, max_val=N_B)
            with act.Fori(N_ALL, N_B) as n:
                with act.If(n < n_tiles):
                    load_x(n, n * P)
                    take_xt(n)
                    silu(n)
                    high_of_hidden(n)
                    take_ht(n)
                    store_d(n)
                with act.Else():
                    act.wait_ge(d_free, n + 1)
                    act.wait_ge(d_out, n * 16)
                    act.dma_start(rows_d[ds(n * P, P), :], dout[:, :]).then_inc(d_out, 16)
                    act.wait_ge(xin_in, n * 16)
                    act.sem_inc(xin_in, 16)
                    for done in (xt_high, silu_done, hid_high, ht_high, d_free):
                        act.sem_inc(done, 1)

            load_x(N_B, 0)
            take_xt(N_B)
            load_x(N_B + 1, P)
            with act.Fori(N_B, N_B + TT - 2) as n:
                tile(n, (n + 2 - N_B) * P)
            tile(N_B + TT - 2)
            tile(N_B + TT - 1, last=True)

        @block.vector
        def _(dve):
            v = nc.vector
            for free in (qin_free, x1_free, logits_free):
                dve.sem_inc(free, 1)

            def blocks(ap):
                return ap.rearrange("p (k n) -> p k n", k=KH)

            def per_block(ap):
                return ap.unsqueeze(2).to_broadcast([P, KH, P])

            step = Chain(dve, gw_step, 0)
            dve.wait_ge(gw_in, 16)
            step(v.tensor_scalar(gw_f[:, :], gw_f[:, :], WSCALE, None, ALU.mult))
            step(v.tensor_copy(gw[:, 0, :], gw_f[:, :]))
            v.tensor_tensor(gw[:, 1, :], gw_f[:, :], gw[:, 0, :], ALU.subtract).then_inc(gw_ready, 1)
            dve.wait_ge(const_ready, CONSTS)

            def guard(step, eps, scale):
                step(v.tensor_scalar(safe[:, :], amax[:, :], eps, None, ALU.max))
                v.tensor_scalar(from_q[:, :], safe[:, :], 1.0 / FP8_MAX, scale, ALU.mult, ALU.mult)
                step(v.reciprocal(to_q[:, :], safe[:, :]))
                step(v.tensor_scalar(to_q[:, :], to_q[:, :], FP8_MAX, None, ALU.mult))

            def quantise(step, src, n, src_free):
                first = v.tensor_tensor(blocks(t0), blocks(src), per_block(to_q[:, :]), ALU.mult)
                if src_free is not None:
                    first.then_inc(src_free, 1)
                    dve.wait_ge(src_free, n + 2)
                else:
                    step(first)
                step(v.tensor_scalar(t1.bitcast(I32), t0.bitcast(I32), EXP_MASK, None, ALU.bitwise_and))
                step(v.tensor_scalar(t1, t1, FP8_MIN_EXP, FP8_ROUND, ALU.max, ALU.mult))
                step(v.tensor_tensor(t0, t0, t1, ALU.add))
                step(v.tensor_tensor(t0, t0, t1, ALU.subtract))
                step(v.tensor_tensor(blocks(t0), blocks(t0), per_block(from_q[:, :]), ALU.mult))
                dve.wait_ge(nat_free, n + 1)
                step(v.tensor_copy(nat[:, 0, :], t0))
                v.tensor_tensor(nat[:, 1, :], t0, nat[:, 0, :], ALU.subtract).then_inc(nat_ready, 1)

            def ctx_tile(c, n):
                step = Chain(dve, ctx_step, c * CTX_STEPS)
                dve.wait_ge(qin_in, n * 16 + 16)
                v.tensor_reduce(amax_p[:, :], blocks(qin), AX.X, ALU.max, apply_absolute_value=True)\
                    .then_inc(block_max, 1)
                dve.wait_ge(block_max_all, c + 1)
                guard(step, W_EPS, WSCALE)
                quantise(step, qin, n, qin_free)
                assert step.n == CTX_STEPS

            def moments(step, src, stats, mv, var):
                v.bn_stats(stats[:, 0:6], src[:, 0:512])
                step(v.bn_stats(stats[:, 6:12], src[:, 512:1024]))
                dve.sem_inc(dve_turn, 1)
                step(v.bn_aggr(mv[:, :], stats[:, :]))
                v.tensor_scalar(var[:, :], mv[:, 1:2], LN_EPS, None, ALU.add).then_inc(var_ready, 1)

            def x_tile(i, n, r):
                step = Chain(dve, x_step, i * X_STEPS)
                dve.wait_ge(qin_in, n * 16 + 16)
                moments(step, qin, stats_q, mv_q, var_q)
                dve.wait_ge(std_ready, r + 1)
                step(v.reciprocal(rstd_q[:, :], std_q[:, :]))
                v.tensor_scalar(t2, qin, mv_q[:, 0:1], rstd_q[:, :], ALU.subtract, ALU.mult).then_inc(qin_free, 1)
                dve.wait_ge(qin_free, n + 2)
                step(v.tensor_reduce(amax[:, :], blocks(t2), AX.X, ALU.max, apply_absolute_value=True))
                guard(step, ACT_EPS, 1.0)
                quantise(step, t2, n, None)
                assert step.n == X_STEPS

            def residual(i, r):
                step = Chain(dve, ln_step, i * LN_STEPS)
                dve.wait_ge(attn_done, i + 1)
                dve.wait_ge(xres_in, i * 16 + 16)
                v.scalar_tensor_tensor(out=x1b, in0=ps_d_flat, scalar=1.0 / WSCALE, in1=xres, op0=ALU.mult,
                                       op1=ALU.add).then_inc(x1_free, 1)
                dve.wait_ge(x1_free, i + 2)
                moments(step, x1b, stats_l, mv_l, var_l)
                dve.wait_ge(std_ready, r + 1)
                step(v.reciprocal(rstd_l[:, :], std_l[:, :]))
                step(v.tensor_scalar(t2, x1b, mv_l[:, 0:1], rstd_l[:, :], ALU.subtract, ALU.mult))
                dve.wait_ge(x2_free, i + 1)
                step(v.tensor_copy(x2nat[:, 0, :], t2))
                v.tensor_tensor(x2nat[:, 1, :], t2, x2nat[:, 0, :], ALU.subtract).then_inc(x2_ready, 1)
                assert step.n == LN_STEPS

            def choose(i):
                step = Chain(dve, top_step, i * TOP_STEPS)
                dve.wait_ge(logits_done, i + 1)
                step(v.tensor_reduce(group8[:, 0:GROUPS], ps_logits.rearrange("p (g e) -> p g e", g=GROUPS), AX.X,
                                     ALU.max))
                dve.sem_inc(dve_turn, 1)
                step(v.max(group_top[:, :], group8[:, :]))
                dve.sem_inc(dve_turn, 1)
                step(v.max_index(group_idx[:, :], group_top[:, :], group8[:, :]))
                step(v.tensor_copy(group_f[:, :], group_idx[:, 0:TOPG]))
                step(v.tensor_scalar(chosen[:, :], iota_e[:, 0:GROUPS], group_f[:, 0:1], None, ALU.is_equal))
                step(v.scalar_tensor_tensor(out=chosen2[:, :], in0=iota_e[:, 0:GROUPS], scalar=group_f[:, 1:2],
                                            in1=chosen[:, :], op0=ALU.is_equal, op1=ALU.add))
                step(v.tensor_scalar(chosen[:, :], chosen2[:, :], -NEG, NEG, ALU.mult, ALU.add))
                v.tensor_tensor(masked[:, :].rearrange("p (g e) -> p g e", g=GROUPS),
                                ps_logits.rearrange("p (g e) -> p g e", g=GROUPS),
                                chosen[:, :].unsqueeze(2).to_broadcast([P, GROUPS, E // GROUPS]),
                                ALU.add).then_inc(logits_free, 1)
                dve.wait_ge(logits_free, i + 2)
                dve.sem_inc(dve_turn, 1)
                step(v.max(expert_top[:, :], masked[:, :]))
                dve.sem_inc(dve_turn, 1)
                step(v.max_index(expert_idx[:, :], expert_top[:, :], masked[:, :]))
                v.tensor_copy(top_w[:, ds(i, 1), :].rearrange("p a k -> p (a k)"), expert_top[:, 0:TOPK])
                step(v.tensor_copy(top_idx[:, ds(i, 1), :].rearrange("p a k -> p (a k)"), expert_idx[:, 0:TOPK]))
                assert step.n == TOP_STEPS

            with dve.Fori(0, B) as b:
                i0, n0, r0 = b * BT, b * (2 * BT), b * (2 * BT)
                with dve.Fori(0, BT) as j:
                    ctx_tile(i0 + j, n0 + j)
                x_tile(i0, n0 + BT, r0)
                x_tile(i0 + 1, n0 + (BT + 1), r0 + 1)
                residual(i0, r0 + 2)
                with dve.Fori(1, BT - 1) as j:
                    x_tile(i0 + j + 1, n0 + j + (BT + 1), r0 + j * 2 + 1)
                    residual(i0 + j, r0 + j * 2 + 2)
                    choose(i0 + j - 1)
                residual(i0 + (BT - 1), r0 + (2 * BT - 1))
                choose(i0 + (BT - 2))
                choose(i0 + (BT - 1))

            dve.sem_inc(top_ready, 1)
            dve.wait_ge(x1_out, 16 * TT)
            dve.wait_ge(x2_out, 16 * TT)
            step = Chain(dve, route_step, 0)
            full = [P, TT, TOPK, E]
            for k in range(TOPK):
                last = v.tensor_tensor(hot[:, :, k, :], top_idx[:, :, k:k + 1].to_broadcast([P, TT, E]),
                                       iota_e[:, :].unsqueeze(1).to_broadcast([P, TT, E]), ALU.is_equal)
            step(last)
            with nc.allow_low_precision(reason="at most one of the six is 1"):
                step(v.tensor_reduce(mask, hot.rearrange("p t k e -> p t e k"), AX.X, ALU.add))
            v.memset(pre_a[:, 0:1, :], 0.0)
            step(v.tensor_copy(pre_a[:, 1:TT, :], mask[:, 0:TT - 1, :]))
            src, dst, d = pre_a, pre_b, 1
            while d < TT:
                v.tensor_copy(dst[:, 0:d, :], src[:, 0:d, :])
                step(v.tensor_tensor(dst[:, d:TT, :], src[:, d:TT, :], src[:, 0:TT - d, :], ALU.add))
                src, dst, d = dst, src, 2 * d
            assert src is pre_b
            dve.sem_inc(mask_ready, 1)
            dve.wait_ge(sig_ready, 1)
            step(v.tensor_reduce(w_sum[:, :], top_w[:, :, :], AX.X, ALU.add))
            step(v.reciprocal(w_sum[:, :], w_sum[:, :]))
            step(v.tensor_tensor(top_w[:, :, :], top_w[:, :, :],
                                 w_sum[:, :].unsqueeze(2).to_broadcast([P, TT, TOPK]), ALU.mult))
            dve.wait_ge(rank_done, 1)
            step(v.tensor_copy(count[:, :], ps_gu[:, 2, 0:E]))
            step(v.tensor_scalar(tiles_e[:, :], count[:, :], P - 1.0, 1.0 / P, ALU.add, ALU.mult))
            step(v.tensor_scalar(tiles_e[:, :], tiles_e[:, :], -127.0 / 256, 2.0 ** 23, ALU.add, ALU.add))
            step(v.tensor_scalar(tiles_e[:, :], tiles_e[:, :], -2.0 ** 23, None, ALU.add))
            step(v.tensor_tensor_scan(ends[:, :], ones_f[:, :], tiles_e[:, :], 0.0, ALU.mult, ALU.add))
            step(v.tensor_tensor(first_slot[:, :], ends[:, :], tiles_e[:, :], ALU.subtract))
            step(v.tensor_scalar(first_slot[:, :], first_slot[:, :], float(P), float(T), ALU.mult, ALU.add))
            step(v.tensor_tensor(place, ps_gu[:, 0:2, :].rearrange("p a (t e) -> p (a t) e", e=E),
                                 first_slot[:, :].unsqueeze(1).to_broadcast([P, TT, E]), ALU.add))
            for k in range(TOPK):
                last = v.tensor_tensor(prod[:, :, k, :], hot[:, :, k, :], place, ALU.mult)
            step(last)
            step(v.tensor_reduce(top_idx[:, :, :], prod, AX.X, ALU.add))
            step(v.tensor_copy(slot[:, :, :], top_idx[:, :, :]))
            step(v.tensor_tensor(tab_cmp, iota_t[0:1, :].unsqueeze(2).to_broadcast([1, SLOT_TILES, E]),
                                 ends[0:1, :].unsqueeze(1).to_broadcast([1, SLOT_TILES, E]), ALU.is_ge))
            step(v.tensor_reduce(expert_t[0:1, :], tab_cmp, AX.X, ALU.add))
            v.memset(ready_tab[0:1, 0:TT], 1)
            v.memset(buf_tab[0:1, 0:TT], 0)
            v.memset(done_tab[0:1, 0:1], 1)
            v.memset(done_tab[0:1, 1:2], TT)
            v.tensor_scalar(done_tab[0:1, 2:E + 2], ends[0:1, :], float(TT), None, ALU.add)
            v.tensor_scalar(count_tab[0:1, :], ends[0:1, E - 1:E], float(TT), None, ALU.add)
            step(v.tensor_scalar(ready_tab[0:1, TT:], expert_t[0:1, :], E - 1.0, 2.0, ALU.min, ALU.add))
            step(v.tensor_scalar(buf_tab[0:1, TT:], ready_tab[0:1, TT:], 1, 1, ALU.bitwise_and, ALU.bitwise_xor))
            step(v.tensor_scalar(tmp_e[:, :], tiles_e[:, :], float(P), iota_p[:, :], ALU.mult, ALU.add))
            step(v.scalar_tensor_tensor(out=tmp_e[:, :], in0=tmp_e[:, :], scalar=-float(P), in1=count[:, :],
                                        op0=ALU.add, op1=ALU.is_ge))
            step(v.tensor_scalar(first_slot[:, :], ends[:, :], float(P), iota_p[:, :], ALU.mult, ALU.add))
            step(v.tensor_scalar(first_slot[:, :], first_slot[:, :], T - P + FAR, None, ALU.add))
            v.scalar_tensor_tensor(out=pad_idx[:, :], in0=tmp_e[:, :], scalar=-FAR, in1=first_slot[:, :],
                                   op0=ALU.mult, op1=ALU.add).then_inc(routed, 1)

            def take_xt(n):
                dve.wait_ge(trx, n + 1)
                v.tensor_copy(xT[:, 1, :, :].rearrange("p k n -> p (k n)"), ps_t[:, 1, :]).then_inc(xt_low, 1)

            def hidden(n):
                dve.wait_ge(silu_done, n + 1)
                v.scalar_tensor_tensor(out=hid[:, :, :], in0=ps_gu[:, 2:4, 0:CH], scalar=HSCALE / WSCALE,
                                       in1=sil[:, :, :], op0=ALU.mult, op1=ALU.mult).then_inc(hid_done, 1)

            def low_of_hidden(n):
                dve.wait_ge(hid_high, n + 1)
                v.tensor_tensor(hid_hl[:, 1, :], hid[:, :, :].rearrange("p a c -> p (a c)"), hid_hl[:, 0, :],
                                ALU.subtract).then_inc(hid_low, 1)

            def take_ht(n):
                dve.wait_ge(trh, n + 1)
                v.tensor_copy(hT[:, 1, 0:KM * P], ps_t[:, 1, 0:KM * P]).then_inc(ht_low, 1)

            def tile(n, last=False, before=None):
                hidden(n)
                if not last:
                    take_xt(n + 1)
                low_of_hidden(n)
                if before is not None:
                    combine(*before)
                take_ht(n)

            def combine(i, u, pair):
                step = Chain(dve, comb_step, i * COMB_STEPS)
                dve.wait_ge(down_done, i + (N_B + 1))
                dve.wait_ge(side_in[u], pair * 32 + 32)
                v.scalar_tensor_tensor(out=total[u], in0=ps_d_flat, scalar=1.0 / (WSCALE * HSCALE), in1=total[u],
                                       op0=ALU.mult, op1=ALU.add).then_inc(d_free, 1)
                dve.wait_ge(d_free, i + (N_B + 2))
                step(v.tensor_tensor(total[u], total[u], a_rows[u], ALU.add))
                dve.wait_ge(gat_in[u], pair * (16 * TOPK) + 16 * TOPK)
                for k in range(TOPK):
                    ins = v.scalar_tensor_tensor(
                        out=total[u], in0=gat[u][:, k, :],
                        scalar=top_w[:, ds(i, 1), k:k + 1].rearrange("p a k -> p (a k)"), in1=total[u],
                        op0=ALU.mult, op1=ALU.add)
                    if k < TOPK - 1:
                        step(ins)
                    else:
                        ins.then_inc(comb_done, 1)
                assert step.n == COMB_STEPS

            take_xt(0)
            with dve.Fori(0, N_ALL - 1) as n:
                tile(n)
            tile(N_ALL - 1, last=True)

            n_tiles = dve.value_load(count_tab[0:1, 0:1], min_val=N_ALL, max_val=N_B)
            with dve.Fori(N_ALL, N_B) as n:
                with dve.If(n < n_tiles):
                    take_xt(n)
                    hidden(n)
                    low_of_hidden(n)
                    take_ht(n)
                with dve.Else():
                    dve.wait_ge(ht_low, n)
                    for done in (xt_low, hid_done, hid_low, ht_low):
                        dve.sem_inc(done, 1)

            take_xt(N_B)
            tile(N_B)
            with dve.Fori(0, TT // 2 - 1) as q:
                tile(q * 2 + (N_B + 1), before=(q * 2, 0, q))
                tile(q * 2 + (N_B + 2), before=(q * 2 + 1, 1, q))
            tile(N_B + TT - 1, last=True, before=(TT - 2, 0, TT // 2 - 1))
            combine(TT - 1, 1, TT // 2 - 1)


_INS = ["x", "ctx_2048", "L0_ffn_gate_w", "L0_ffn_w_gate", "L0_ffn_w_up", "L0_ffn_w_down", "L0_ffn_sw_gate",
        "L0_ffn_sw_up", "L0_ffn_sw_down"]


def kernel(**inputs):
    import numpy as _np
    import concourse.bacc as _bacc
    from concourse.bass_utils import run_bass_kernel_spmd as _run

    nc = _bacc.Bacc("TRN2", target_bir_lowering=False, num_devices=1)
    arrays, args = {}, []
    for name in _INS:
        a = _np.ascontiguousarray(inputs[name])
        arrays[f"in_{name}"] = a
        args.append(nc.dram_tensor(f"in_{name}", a.shape, mybir.dt.from_np(a.dtype), kind="ExternalInput").ap())
    out = nc.dram_tensor("out_0", (B, S, H), F32, kind="ExternalOutput").ap()
    build(nc, *args, out)
    r = _run(nc, [arrays], core_ids=[0])
    return r.results[0]["out_0"]
```

```python
from contextlib import ExitStack

import concourse.bass as bass
from concourse import mybir

F32 = mybir.dt.float32
F16 = mybir.dt.float16
I32 = mybir.dt.int32
U32 = mybir.dt.uint32
ALU = mybir.AluOpType
ACT = mybir.ActivationFunctionType
AX = mybir.AxisListType
ds = bass.ds

P = 128
B, S, H = 4, 1024, 1024
E, TOPK, GROUPS, TOPG = 32, 6, 4, 2
M = 704
KH = H // P
KM = -(-M // P)
M_LAST = M - (KM - 1) * P
T = B * S
TT = T // P
BT = S // P
CH = M // 2
FULL = T * TOPK // P
EXTRA = E - 1
SLOT_TILES = FULL + EXTRA
GU = KH * 2 * M
WCOLS = GU + KM * H
CHUNKS = KH + KM
STAGES = 4

FP8_MAX, ACT_EPS, W_EPS, LN_EPS = 448.0, 1e-4, 1e-6, 1e-5
EXP_MASK = 0x7F800000
FP8_MIN_EXP = 2.0 ** -6
FP8_ROUND = 1.5 * 2.0 ** 20
WSCALE = 256.0
HSCALE = 16.0
FAR = 2.0 ** 20
NEG = -1.0e30



class Chain:

    def __init__(self, engine, sem, base):
        self.engine, self.sem, self.base, self.n = engine, sem, base, 0

    def __call__(self, instruction):
        self.n += 1
        instruction.then_inc(self.sem, 1)
        self.engine.wait_ge(self.sem, self.base + self.n)


def build(nc, x, ctx_in, gate_w, w_gate, w_up, w_down, sw_gate, sw_up, sw_down, out):
    x_rows = x.rearrange("b s d -> (b s) d")
    c_rows = ctx_in.rearrange("b s d -> (b s) d")
    o_rows = out.rearrange("b s d -> (b s) d")

    rows_x = nc.dram_tensor("rows_x", (T + SLOT_TILES * P, 2 * H), F16).ap()
    rows_d = nc.dram_tensor("rows_d", (T + SLOT_TILES * P, H), F32).ap()
    rows_x1 = nc.dram_tensor("rows_x1", (T, H), F32).ap()
    last_row = T + SLOT_TILES * P - 1

    with ExitStack() as stack:
        def sb(name, shape, dt):
            return stack.enter_context(nc.sbuf_tensor(name, shape, dt))

        def psum(name, shape, dt):
            return stack.enter_context(nc.psum_tensor(name, shape, dt))

        def sem(name):
            return stack.enter_context(nc.semaphore(name))

        wts = sb("wts", [P, 2, 2, WCOLS], F16)
        stage = sb("stage", [P, STAGES, 2 * M], F32)
        xin = sb("xin", [P, 2, H], F16)
        xT = sb("xT", [P, 2, KH, P], F16)
        sil = sb("sil", [P, 2, CH], F32)
        hid = sb("hid", [P, 2, CH], F32)
        hid_hl = sb("hid_hl", [P, 2, M], F16)
        hT = sb("hT", [P, 2, H], F16)
        dout = sb("dout", [P, H], F32)
        ident = sb("ident", [P, P], F16)
        upper = sb("upper", [P, P], F16)
        ones = sb("ones", [P, P], F16)
        ones_f = sb("ones_f", [P, E], F32)
        gw_f = sb("gw_f", [P, KH * E], F32)
        gw = sb("gw", [P, 2, KH * E], F16)
        iota_e = sb("iota_e", [P, E], F32)
        iota_p = sb("iota_p", [P, 1], F32)
        iota_t = sb("iota_t", [P, SLOT_TILES], F32)
        amax_p, amax = (sb(n, [P, 2, KH], F32) for n in ("amax_p", "amax"))
        safe, to_q, from_q = (sb(n, [P, KH], F32) for n in ("safe", "to_q", "from_q"))
        stats_q, mv_q, stats_l, mv_l = (sb(n, [P, w], F32) for n, w in (
            ("stats_q", 12), ("mv_q", 4), ("stats_l", 12), ("mv_l", 2)))
        var_q, std_q, scale_q, shift_q = (sb(n, [P, 2], F32) for n in ("var_q", "std_q", "scale_q", "shift_q"))
        var_l, std_l, scale_l, shift_l = (sb(n, [P, 1], F32) for n in ("var_l", "std_l", "scale_l", "shift_l"))
        group8, group_top, expert_top = (sb(n, [P, 8], F32) for n in ("group8", "group_top", "expert_top"))
        group_idx, expert_idx = sb("group_idx", [P, 8], U32), sb("expert_idx", [P, 8], U32)
        group_f = sb("group_f", [P, TOPG], F32)
        chosen, chosen2 = sb("chosen", [P, GROUPS], F32), sb("chosen2", [P, GROUPS], F32)
        masked = sb("masked", [P, E], F32)
        top_idx = sb("top_idx", [P, TT, TOPK], F32)
        top_w = sb("top_w", [P, TT, TOPK], F32)
        w_sum = sb("w_sum", [P, TT], F32)
        slot = sb("slot", [P, TT, TOPK], I32)
        count = sb("count", [P, E], F32)
        tiles_e, ends, first_slot, tmp_e = (sb(n, [P, E], F32) for n in ("tiles_e", "ends", "first_slot", "tmp_e"))
        expert_t = sb("expert_t", [1, SLOT_TILES], F32)
        ready_tab = sb("ready_tab", [1, TT + SLOT_TILES], I32)
        buf_tab = sb("buf_tab", [1, TT + SLOT_TILES], I32)
        done_tab = sb("done_tab", [1, E + 2], I32)
        count_tab = sb("count_tab", [1, 1], I32)
        pad_idx = sb("pad_idx", [P, E], I32)
        pad_now = sb("pad_now", [P, 4], I32)
        slot_now = sb("slot_now", [P, 2, TOPK], I32)

        early = wts[:, 1, :, :].rearrange("p a c -> p (a c)")
        cT = early[:, 0:2 * KH * S].rearrange("p (a k n) -> p a k n", a=2, k=KH)
        xqT = xin[:, :, :].rearrange("p a (k n) -> p a k n", k=KH)
        e0 = 2 * KH * S
        qin0, qin1, xres, x1b, deq0, deq1, rnd = (
            early[:, e0 + 2 * H * i:e0 + 2 * H * (i + 1)].bitcast(F32) for i in range(7))
        qin, deq = (qin0, qin1), (deq0, deq1)
        nat = early[:, e0 + 2 * H * 7:e0 + 2 * H * 8].rearrange("p (a d) -> p a d", a=2)
        x2nat = early[:, e0 + 2 * H * 8:e0 + 2 * H * 9].rearrange("p (a d) -> p a d", a=2)
        x2f = dout[:, :]
        n_hot = 2 * TT * TOPK * E
        hot, prod = (early[:, i * n_hot:(i + 1) * n_hot].bitcast(F32).rearrange("p (t k e) -> p t k e", t=TT, k=TOPK)
                     for i in range(2))
        mask, pre_a, pre_b = (early[:, 2 * n_hot + TT * E * i:2 * n_hot + TT * E * (i + 1)]
                              .rearrange("p (t e) -> p t e", t=TT) for i in range(3))
        place = early[:, 2 * n_hot + TT * E * 3:2 * n_hot + TT * E * 5].bitcast(F32).rearrange("p (t e) -> p t e", t=TT)
        tab_cmp = early[0:1, 0:2 * SLOT_TILES * E].bitcast(F32).rearrange("p (t e) -> p t e", t=SLOT_TILES)
        xsc = [early[:, 2 * H * i:2 * H * (i + 1)] for i in range(2)]
        zeros = early[:, 4 * H:6 * H]
        late = wts[:, 0, :, :].rearrange("p a c -> p (a c)").bitcast(F32)
        gat = [late[:, u * TOPK * H:(u + 1) * TOPK * H].rearrange("p (k d) -> p k d", k=TOPK) for u in range(2)]
        total = [late[:, (2 * TOPK + u) * H:(2 * TOPK + u + 1) * H] for u in range(2)]
        a_rows = [late[:, (2 * TOPK + 2 + u) * H:(2 * TOPK + 3 + u) * H] for u in range(2)]

        ps_t = psum("ps_t", [P, 2, H], F16)
        ps_gu = psum("ps_gu", [P, 4, 512], F32)
        ps_d = psum("ps_d", [P, 2, 512], F32)
        ps_d_flat = ps_d[:, :, :].rearrange("p a n -> p (a n)")
        ps_logits = ps_gu[:, 0, 0:E]

        const_ready, pool_step, gw_in, gw_step, gw_ready = (sem(n) for n in (
            "const_ready", "pool_step", "gw_in", "gw_step", "gw_ready"))
        conv_step, conv_done, weights_ready = (sem(n) for n in ("conv_step", "conv_done", "weights_ready"))
        qin_in = [sem(f"qin_in{u}") for u in range(2)]
        qin_free, xres_in, block_max, block_max_all = (sem(n) for n in (
            "qin_free", "xres_in", "block_max", "block_max_all"))
        var_q_ready, std_q_ready, scale_q_ready, norm_q = (sem(n) for n in (
            "var_q_ready", "std_q_ready", "scale_q_ready", "norm_q"))
        var_l_ready, std_l_ready, scale_l_ready, norm_l = (sem(n) for n in (
            "var_l_ready", "std_l_ready", "scale_l_ready", "norm_l"))
        deq_ready, nat_high, nat_ready, x1_free, x2_high, x2_ready = (sem(n) for n in (
            "deq_ready", "nat_high", "nat_ready", "x1_free", "x2_high", "x2_ready"))
        tr_done, tr_free, attn_done, logits_done, logits_free, x1_out, x2_out = (sem(n) for n in (
            "tr_done", "tr_free", "attn_done", "logits_done", "logits_free", "x1_out", "x2_out"))
        ctx_step, mean_step, scale_step, x_step, ln_step, top_step = (sem(n) for n in (
            "ctx_step", "mean_step", "scale_step", "x_step", "ln_step", "top_step"))
        route_step, top_ready, sig_ready, mask_ready, rank_done, routed, pad_out = (sem(n) for n in (
            "route_step", "top_ready", "sig_ready", "mask_ready", "rank_done", "routed", "pad_out"))
        xin_in, trx, xt_high, xt_low, gu_done, silu_done = (sem(n) for n in (
            "xin_in", "trx", "xt_high", "xt_low", "gu_done", "silu_done"))
        hid_done, hid_high, hid_low, trh, ht_high, ht_low, down_done, d_free, d_out = (sem(n) for n in (
            "hid_done", "hid_high", "hid_low", "trh", "ht_high", "ht_low", "down_done", "d_free", "d_out"))
        pe_turn, dve_turn, pool_turn = (sem(n) for n in ("pe_turn", "dve_turn", "pool_turn"))
        comb_step, comb_done, o_out = (sem(n) for n in ("comb_step", "comb_done", "o_out"))
        stage_in = [sem(f"stage_in{i}") for i in range(STAGES)]
        xsc_in = [sem(f"xsc_in{u}") for u in range(2)]
        scat_out = [sem(f"scat_out{u}") for u in range(2)]
        gat_in = [sem(f"gat_in{u}") for u in range(2)]
        side_in = [sem(f"side_in{u}") for u in range(2)]

        CONSTS = 9
        SETS = 3 * BT
        LEAD = 3
        N_ALL = TT + FULL
        N_B = TT + SLOT_TILES
        A_LAST = TT - 2
        CTX_STEPS, MEAN_STEPS, X_STEPS, LN_STEPS, TOP_STEPS, COMB_STEPS = 7, 2, 8, 3, 10, 6

        def stage_of(o, c):
            return (o * CHUNKS + c) % STAGES

        def loads_of(o, c):
            return sum((g % STAGES) == stage_of(o, c) for g in range(o * CHUNKS + c + 1))

        def set_of_x(j):
            return BT if isinstance(j, int) and j == 0 else j * 2 + (BT - 1)

        def set_of_x2(j):
            return j * 2 + (BT + 2)

        pair_loads = [sum(g % STAGES == st for g in range(2 * CHUNKS)) for st in range(STAGES)]

        block = stack.enter_context(nc.Block())

        @block.sync
        def _(sp):
            def load_piece(o, c, gate, up, down):
                st = stage_of(o, c)
                if c < KH:
                    sp.dma_start(stage[:, st, 0:M], gate[c * P:(c + 1) * P, :]).then_inc(stage_in[st], 16)
                    sp.dma_start(stage[:, st, M:2 * M], up[c * P:(c + 1) * P, :]).then_inc(stage_in[st], 16)
                else:
                    r0 = (c - KH) * P
                    n = min(P, M - r0)
                    for h in range(2):
                        sp.dma_start(stage[0:n, st, h * 512:(h + 1) * 512],
                                     down[r0:r0 + n, h * 512:(h + 1) * 512]).then_inc(stage_in[st], 16)

            half_a = (sw_gate[:, 0:M], sw_up[:, 0:M], sw_down[0:M, :])
            half_b = (sw_gate[:, M:2 * M], sw_up[:, M:2 * M], sw_down[M:2 * M, :])
            sp.dma_start(gw_f[:, :].rearrange("p (k e) -> p k e", k=KH),
                         gate_w.rearrange("(k p) e -> p k e", p=P)).then_inc(gw_in, 16)
            for c in range(STAGES):
                load_piece(0, c, *half_a)

            def load_q(rows, row, n, u):
                sp.wait_ge(qin_free, n)
                sp.dma_start(qin[u], rows[ds(row, P), :]).then_inc(qin_in[u], 16)

            def load_res(i):
                sp.wait_ge(x1_free, i + 1)
                sp.dma_start(xres, x_rows[ds(i * P, P), :]).then_inc(xres_in, 16)

            def store_x1(i):
                sp.wait_ge(x1_free, i + 2)
                sp.dma_start(rows_x1[ds(i * P, P), :], x1b).then_inc(x1_out, 16)

            def store_x2(i):
                sp.wait_ge(x2_ready, i + 1)
                sp.dma_start(rows_x[ds(i * P, P), :], x2nat.rearrange("p a d -> p (a d)")).then_inc(x2_out, 16)

            with sp.Fori(0, B) as b:
                i0, n0 = b * BT, b * (2 * BT)
                with sp.Fori(0, BT // 2) as q:
                    for u in range(2):
                        load_q(c_rows, (i0 + q * 2 + u) * P, n0 + q * 2 + u, u)
                for j in range(LEAD + 2):
                    load_q(x_rows, (i0 + j) * P, n0 + (BT + j), j % 2)
                    if j == 0:
                        load_res(i0)
                for j in range(BT - LEAD - 2):
                    store_x1(i0 + j)
                    load_res(i0 + (j + 1))
                    load_q(x_rows, (i0 + (j + LEAD + 2)) * P, n0 + (BT + j + LEAD + 2), (j + LEAD) % 2)
                    store_x2(i0 + j)
                with sp.Fori(BT - LEAD - 2, BT - 1) as j:
                    store_x1(i0 + j)
                    load_res(i0 + j + 1)
                    store_x2(i0 + j)
                store_x1(i0 + (BT - 1))
                store_x2(i0 + (BT - 1))

            for c in range(STAGES, CHUNKS):
                sp.wait_ge(conv_done, c - STAGES + 1)
                load_piece(0, c, *half_a)

            sp.wait_ge(routed, 1)
            for u in range(2):
                sp.dma_start(xsc[u], rows_x[u * P:(u + 1) * P, :]).then_inc(xsc_in[u], 16)
            with sp.Fori(1, TT // 2) as q:
                for u in range(2):
                    sp.wait_ge(scat_out[u], q * (16 * TOPK))
                    sp.dma_start(xsc[u], rows_x[ds((q * 2 + u) * P, P), :]).then_inc(xsc_in[u], 16)

            with sp.Fori(0, E // 2) as q:
                for u in range(2):
                    mats = [w[ds(q * 2 + u, 1)].rearrange("a r c -> (a r) c") for w in (w_gate, w_up, w_down)]
                    for c in range(CHUNKS):
                        sp.wait_ge(conv_done, q * (2 * CHUNKS) + ((1 + u) * CHUNKS + c - STAGES + 1))
                        load_piece(1 + u, c, *mats)
            for c in range(CHUNKS):
                sp.wait_ge(conv_done, (E + 1) * CHUNKS + c - STAGES + 1)
                load_piece(1, c, *half_b)

            sp.wait_ge(down_done, N_B)
            sp.wait_ge(d_out, 16 * N_B)

            def side(i, u):
                sp.dma_start(total[u], rows_x1[ds(i * P, P), :]).then_inc(side_in[u], 16)
                sp.dma_start(a_rows[u], rows_d[ds(i * P, P), :]).then_inc(side_in[u], 16)

            def store_out(i, u):
                sp.wait_ge(comb_done, i + 1)
                sp.dma_start(o_rows[ds(i * P, P), :], total[u]).then_inc(o_out, 16)

            side(0, 0)
            side(1, 1)
            with sp.Fori(0, TT // 2 - 1) as q:
                for u in range(2):
                    store_out(q * 2 + u, u)
                    sp.wait_ge(o_out, q * 32 + 16 * (u + 1))
                    side(q * 2 + u + 2, u)
            store_out(TT - 2, 0)
            store_out(TT - 1, 1)
            sp.wait_ge(o_out, 16 * TT)

        @block.gpsimd
        def _(pool):
            g = nc.gpsimd
            g.memset(ident[:, :], 0.0).then_inc(pool_step, 1)
            g.memset(upper[:, :], 1.0).then_inc(pool_step, 1)
            g.memset(ones[:, :], 1.0).then_inc(const_ready, 1)
            g.memset(ones_f[:, :], 1.0).then_inc(const_ready, 1)
            g.memset(group8[:, :], -3.0e38).then_inc(const_ready, 1)
            pool.wait_ge(pool_step, 2)
            g.affine_select(out=ident[:, :], in_=ident[:, :], compare_op=ALU.not_equal, fill=1.0, base=0,
                            pattern=[[-1, P]], channel_multiplier=1).then_inc(const_ready, 1)
            g.affine_select(out=upper[:, :], in_=upper[:, :], compare_op=ALU.is_gt, fill=0.0, base=0,
                            pattern=[[1, P]], channel_multiplier=-1).then_inc(const_ready, 1)
            g.iota(iota_e[:, :], pattern=[[1, E]], base=0, channel_multiplier=0,
                   allow_small_or_imprecise_dtypes=True).then_inc(const_ready, 1)
            g.iota(iota_p[:, :], pattern=[[0, 1]], base=0, channel_multiplier=1,
                   allow_small_or_imprecise_dtypes=True).then_inc(const_ready, 1)
            g.iota(iota_t[:, :], pattern=[[1, SLOT_TILES]], base=0, channel_multiplier=0,
                   allow_small_or_imprecise_dtypes=True).then_inc(const_ready, 1)
            g.memset(amax[:, :, :], 0.0).then_inc(const_ready, 1)
            pool.sem_inc(nat_ready, 1)

            def split_piece(o, c, buf, pair=0):
                st = stage_of(o, c)
                n, cols, at = (P, 2 * M, c * 2 * M) if c < KH else \
                    (min(P, M - (c - KH) * P), H, GU + (c - KH) * H)
                high, low = wts[0:n, buf, 0, at:at + cols], wts[0:n, buf, 1, at:at + cols]
                raw = stage[0:n, st, 0:cols]
                step = pair * (4 * CHUNKS) + 2 * (o * CHUNKS + c)
                pool.wait_ge(stage_in[st], pair * (32 * pair_loads[st]) + 32 * loads_of(o, c))
                pool.sem_inc(pool_turn, 1)
                g.tensor_scalar(high, raw, WSCALE, 1.0, ALU.mult, ALU.mult).then_inc(conv_step, 1)
                g.tensor_scalar(raw, raw, WSCALE, 1.0, ALU.mult, ALU.mult).then_inc(conv_step, 1)
                pool.wait_ge(conv_step, step + 2)
                g.tensor_tensor(low, raw, high, ALU.subtract).then_inc(conv_done, 1)

            for c in range(STAGES):
                split_piece(0, c, 0)

            def all_max(c, u):
                pool.wait_ge(block_max, c + 1)
                pool.sem_inc(pool_turn, 1)
                g.partition_all_reduce(amax[:, u, :], amax_p[:, u, :], P,
                                       bass.bass_isa.ReduceOp.max).then_inc(block_max_all, 1)

            def low_of_nat(n, u):
                pool.wait_ge(nat_high, n + 1)
                g.tensor_tensor(nat[:, 1, :], deq[u], nat[:, 0, :], ALU.subtract).then_inc(nat_ready, 1)

            def low_of_x2(i):
                pool.wait_ge(x2_high, i + 1)
                g.tensor_tensor(x2nat[:, 1, :], x2f, x2nat[:, 0, :], ALU.subtract).then_inc(x2_ready, 1)

            with pool.Fori(0, B) as b:
                i0, n0 = b * BT, b * (2 * BT)
                all_max(i0, 0)
                with pool.Fori(0, BT // 2 - 1) as q:
                    for u in range(2):
                        all_max(i0 + q * 2 + (u + 1), 1 - u)
                        low_of_nat(n0 + q * 2 + u, u)
                all_max(i0 + (BT - 1), 1)
                for c in range(BT - 2, BT + LEAD - 1):
                    low_of_nat(n0 + c, c % 2)
                with pool.Fori(0, (BT - LEAD + 1) // 2) as q:
                    for u in range(2):
                        low_of_nat(n0 + q * 2 + (BT + LEAD - 1 + u), u)
                        low_of_x2(i0 + q * 2 + u)
                with pool.Fori(BT - LEAD + 1, BT) as j:
                    low_of_x2(i0 + j)
            for c in range(STAGES, CHUNKS):
                split_piece(0, c, 0)
            pool.wait_ge(conv_done, CHUNKS)
            pool.sem_inc(weights_ready, 1)

            pool.wait_ge(routed, 1)
            g.memset(zeros, 0.0).then_inc(pool_step, 1)
            pool.wait_ge(pool_step, 3)

            def pad_four(q):
                g.tensor_copy(pad_now[:, :], pad_idx[:, ds(q * 4, 4)]).then_inc(pool_step, 1)
                pool.wait_ge(pool_step, q + 4)
                pool.sem_inc(pool_turn, 1)
                for u in range(4):
                    g.indirect_dma_start(
                        out=rows_x, out_offset=bass.IndirectOffsetOnAxis(ap=pad_now[:, u:u + 1], axis=0),
                        in_=zeros, in_offset=None, bounds_check=last_row, oob_is_err=False).then_inc(pad_out, 16)

            pad_four(0)
            with pool.Fori(1, E // 4) as q:
                pool.wait_ge(pad_out, q * 64)
                pad_four(q)

            with pool.Fori(0, TT // 2) as q:
                for u in range(2):
                    pool.wait_ge(xsc_in[u], q * 16 + 16)
                    g.tensor_copy(slot_now[:, u, :], slot[:, ds(q * 2 + u, 1), :].rearrange("p a k -> p (a k)")
                                  ).then_inc(pool_step, 1)
                    pool.wait_ge(pool_step, q * 2 + (u + 4 + E // 4))
                    pool.sem_inc(pool_turn, 1)
                    for k in range(TOPK):
                        g.indirect_dma_start(
                            out=rows_x, out_offset=bass.IndirectOffsetOnAxis(ap=slot_now[:, u, k:k + 1], axis=0),
                            in_=xsc[u], in_offset=None, bounds_check=last_row,
                            oob_is_err=False).then_inc(scat_out[u], 16)
            pool.wait_ge(pad_out, 16 * E)
            for u in range(2):
                pool.wait_ge(scat_out[u], 16 * TOPK * TT // 2)

            with pool.Fori(0, E // 2) as q:
                for u in range(2):
                    done = pool.value_load(done_tab[0:1, ds(q * 2 + u, 1)], min_val=1, max_val=N_B)
                    pool.wait_ge(down_done, done)
                    pool.sem_inc(pool_turn, 1)
                    for c in range(CHUNKS):
                        split_piece(1 + u, c, 1 - u, q)
                    pool.wait_ge(conv_done, q * (2 * CHUNKS) + (2 + u) * CHUNKS)
                    pool.sem_inc(weights_ready, 1)
            done = pool.value_load(done_tab[0:1, E:E + 1], min_val=1, max_val=N_B)
            pool.wait_ge(down_done, done)
            pool.sem_inc(pool_turn, 1)
            for c in range(CHUNKS):
                split_piece(1, c, 1, E // 2)
            pool.wait_ge(conv_done, (E + 2) * CHUNKS)
            pool.sem_inc(weights_ready, 1)

            pool.wait_ge(down_done, N_B)
            pool.wait_ge(d_out, 16 * N_B)

            def gather(i, u, step):
                g.tensor_copy(slot_now[:, u, :], slot[:, ds(i, 1), :].rearrange("p a k -> p (a k)")
                              ).then_inc(pool_step, 1)
                pool.wait_ge(pool_step, step)
                pool.sem_inc(pool_turn, 1)
                for k in range(TOPK):
                    g.indirect_dma_start(
                        out=gat[u][:, k, :], out_offset=None, in_=rows_d,
                        in_offset=bass.IndirectOffsetOnAxis(ap=slot_now[:, u, k:k + 1], axis=0),
                        bounds_check=last_row, oob_is_err=False).then_inc(gat_in[u], 16)

            step0 = 3 + E // 4 + TT
            gather(0, 0, step0 + 1)
            gather(1, 1, step0 + 2)
            with pool.Fori(1, TT // 2) as q:
                for u in range(2):
                    pool.wait_ge(comb_done, q * 2 + (u - 1))
                    gather(q * 2 + u, u, q * 2 + (u + 1 + step0))

        @block.tensor
        def _(pe):
            def transposes(src, blocks, width_last=P):
                for a in range(2):
                    for k in range(blocks):
                        w = width_last if k == blocks - 1 else P
                        last = nc.tensor.transpose(ps_t[0:w, a, k * P:(k + 1) * P], src[:, a, k * P:k * P + w],
                                                   ident[:, :])
                return last

            def three(dst, high, low, w_high, w_low, first, last):
                n = len(dst)
                for a, (left, right) in enumerate(((high, w_high), (high, w_low), (low, w_high))):
                    for c in range(n):
                        ins = nc.tensor.matmul(dst[c], left, right[c], start=(first and a == 0),
                                               stop=(last and a == 2))
                return ins

            pe.wait_ge(const_ready, CONSTS)
            pe.wait_ge(gw_ready, 1)

            def tr(src, t, ready, n):
                pe.wait_ge(ready, n)
                pe.wait_ge(tr_free, t + 1)
                transposes(src, KH).then_inc(tr_done, 1)

            def tr_ctx(b, j):
                tr(nat, b * SETS + j, nat_ready, b * (2 * BT) + j + 2)

            def tr_q(b, j):
                tr(nat, b * SETS + set_of_x(j), nat_ready, b * (2 * BT) + j + (BT + 2))

            def tr_x2(b, j, t):
                tr(x2nat, b * SETS + t, x2_ready, b * BT + j + 1)

            def attend(b, j, x2_too):
                pe.wait_ge(tr_free, b * SETS + set_of_x(j) + 2)
                pe.wait_ge(x1_free, b * BT + j + 1)
                for k in range(KH):
                    if x2_too and k == KH - 2:
                        tr_x2(b, j - 1, set_of_x2(j - 1))
                    ins = three([ps_d[:, c, :] for c in range(2)], xqT[:, 0, k, :], xqT[:, 1, k, :],
                                [cT[:, 0, k, c * 512:(c + 1) * 512] for c in range(2)],
                                [cT[:, 1, k, c * 512:(c + 1) * 512] for c in range(2)], k == 0, k == KH - 1)
                ins.then_inc(attn_done, 1)

            def logits(b, j, t):
                pe.wait_ge(tr_free, b * SETS + t + 2)
                pe.wait_ge(logits_free, b * BT + j + 1)
                for k in range(KH):
                    ins = three([ps_logits], xT[:, 0, k, :], xT[:, 1, k, :], [gw[:, 0, k * E:(k + 1) * E]],
                                [gw[:, 1, k * E:(k + 1) * E]], k == 0, k == KH - 1)
                ins.then_inc(logits_done, 1)

            with pe.Fori(0, B) as b:
                with pe.Fori(0, BT) as j:
                    tr_ctx(b, j)
                tr_q(b, 0)
                attend(b, 0, False)
                tr_q(b, 1)
                with pe.Fori(1, BT - 1) as j:
                    attend(b, j, True)
                    tr_q(b, j + 1)
                    logits(b, j - 1, set_of_x2(j - 1))
                attend(b, BT - 1, True)
                logits(b, BT - 2, set_of_x2(BT - 2))
                tr_x2(b, BT - 1, SETS - 1)
                logits(b, BT - 1, SETS - 1)

            pe.wait_ge(mask_ready, 1)
            half = TT // 2
            for c in range(2):
                nc.tensor.matmul(ps_gu[:, c, :], upper[:, :],
                                 mask[:, c * half:(c + 1) * half, :].rearrange("p t e -> p (t e)"),
                                 start=True, stop=False)
                nc.tensor.matmul(ps_gu[:, c, :], ones[:, :],
                                 pre_b[:, c * half:(c + 1) * half, :].rearrange("p t e -> p (t e)"),
                                 start=False, stop=True)
            nc.tensor.matmul(ps_gu[:, 2, 0:E], ones[:, :], mask[:, TT - 1, :], start=True, stop=False)
            nc.tensor.matmul(ps_gu[:, 2, 0:E], ones[:, :], pre_b[:, TT - 1, :], start=False,
                             stop=True).then_inc(rank_done, 1)
            pe.wait_ge(routed, 1)

            def tr_x(n):
                pe.wait_ge(xin_in, n * 16 + 16)
                transposes(xin, KH).then_inc(trx, 1)

            def gate_up(n, buf):
                for k in range(KH):
                    cols = [k * 2 * M + c * CH for c in range(4)]
                    ins = three([ps_gu[:, c, 0:CH] for c in range(4)], xT[:, 0, k, :], xT[:, 1, k, :],
                                [wts[:, buf, 0, a:a + CH] for a in cols],
                                [wts[:, buf, 1, a:a + CH] for a in cols], k == 0, k == KH - 1)
                ins.then_inc(gu_done, 1)

            def tr_h(n):
                pe.wait_ge(hid_high, n + 1)
                pe.wait_ge(hid_low, n + 1)
                transposes(hid_hl, KM, M_LAST).then_inc(trh, 1)

            def down(n, buf):
                for k in range(KM):
                    r = P if k < KM - 1 else M_LAST
                    cols = [GU + k * H + c * 512 for c in range(2)]
                    ins = three([ps_d[:, c, :] for c in range(2)], hT[0:r, 0, k * P:(k + 1) * P],
                                hT[0:r, 1, k * P:(k + 1) * P],
                                [wts[0:r, buf, 0, a:a + 512] for a in cols],
                                [wts[0:r, buf, 1, a:a + 512] for a in cols], k == 0, k == KM - 1)
                ins.then_inc(down_done, 1)

            def buffer_of(n):
                return pe.value_load(buf_tab[0:1, ds(n, 1)], min_val=0, max_val=1)

            def by_buffer(product, n, which):
                if isinstance(which, int):
                    product(n, which)
                    return
                with pe.If(which < 1):
                    product(n, 0)
                with pe.Else():
                    product(n, 1)

            def weights_of(n, ready):
                if ready is None:
                    ready = pe.value_load(ready_tab[0:1, ds(n, 1)], min_val=1, max_val=E + 1)
                pe.wait_ge(weights_ready, ready)

            def tile(n, buf=None, ready=None, first=False, last=False, buf_before=None):
                if buf is None:
                    buf = buffer_of(n)
                if buf_before is None and not first:
                    buf_before = buffer_of(n - 1)
                weights_of(n, ready)
                pe.wait_ge(xt_high, n + 1)
                pe.wait_ge(xt_low, n + 1)
                if not first:
                    pe.wait_ge(hid_done, n)
                by_buffer(gate_up, n, buf)
                if not first:
                    pe.wait_ge(ht_high, n)
                    pe.wait_ge(ht_low, n)
                if not last:
                    tr_x(n + 1)
                if not first:
                    pe.wait_ge(d_free, n)
                    by_buffer(down, n - 1, buf_before)
                if not last:
                    pe.wait_ge(xt_high, n + 2)
                    pe.wait_ge(xt_low, n + 2)
                tr_h(n)

            def drain_tile(n, buf=None):
                if buf is None:
                    buf = buffer_of(n)
                pe.wait_ge(ht_high, n + 1)
                pe.wait_ge(ht_low, n + 1)
                pe.wait_ge(d_free, n + 1)
                by_buffer(down, n, buf)

            pe.wait_ge(tr_free, B * SETS + 1)
            tr_x(0)
            tile(0, 0, 1, first=True)
            with pe.Fori(1, N_ALL - 1) as n:
                tile(n)
            tile(N_ALL - 1, last=True)
            drain_tile(N_ALL - 1)

            n_tiles = pe.value_load(count_tab[0:1, 0:1], min_val=N_ALL, max_val=N_B)
            with pe.Fori(N_ALL, N_B) as n:
                with pe.If(n < n_tiles):
                    tr_x(n)
                    buf = buffer_of(n)
                    weights_of(n, None)
                    pe.wait_ge(xt_high, n + 1)
                    pe.wait_ge(xt_low, n + 1)
                    by_buffer(gate_up, n, buf)
                    tr_h(n)
                    drain_tile(n, buf)
                with pe.Else():
                    pe.wait_ge(down_done, n)
                    for done in (trx, gu_done, trh, down_done):
                        pe.sem_inc(done, 1)

            tr_x(N_B)
            tile(N_B, 1, E + 2, first=True)
            with pe.Fori(N_B + 1, N_B + TT - 1) as n:
                tile(n, 1, E + 2, buf_before=1)
            tile(N_B + TT - 1, 1, E + 2, last=True, buf_before=1)
            drain_tile(N_B + TT - 1, 1)

        @block.scalar
        def _(act):
            a = nc.scalar
            act.sem_inc(tr_free, 1)
            act.sem_inc(d_free, 1)

            def take(high, low, t):
                act.wait_ge(tr_done, t + 1)
                a.activation(high, ps_t[:, 0, :].rearrange("p (k n) -> p k n", k=KH), ACT.Copy)
                a.activation(low, ps_t[:, 1, :].rearrange("p (k n) -> p k n", k=KH), ACT.Copy).then_inc(tr_free, 1)

            def take_ctx(b, j):
                cols = [cT[:, h, :, ds(j * P, P)] for h in range(2)]
                take(cols[0], cols[1], b * SETS + j)

            def take_q(b, j):
                take(xqT[:, 0], xqT[:, 1], b * SETS + set_of_x(j))

            def take_x2(b, t):
                take(xT[:, 0], xT[:, 1], b * SETS + t)

            def high_of_nat(n, t, u):
                act.wait_ge(deq_ready, n + 1)
                act.wait_ge(tr_done, t)
                a.activation(nat[:, 0, :], deq[u], ACT.Copy).then_inc(nat_high, 1)

            def root_q(i, u):
                act.wait_ge(var_q_ready, i + 1)
                a.activation(std_q[:, u:u + 1], var_q[:, u:u + 1], ACT.Sqrt).then_inc(std_q_ready, 1)

            def normalise_q(i, u):
                act.wait_ge(scale_q_ready, i + 1)
                a.activation(qin[u], qin[u], ACT.Identity, scale=scale_q[:, u:u + 1],
                             bias=shift_q[:, u:u + 1]).then_inc(norm_q, 1)

            def root_l(i):
                act.wait_ge(var_l_ready, i + 1)
                a.activation(std_l[:, :], var_l[:, :], ACT.Sqrt).then_inc(std_l_ready, 1)

            def normalise_l(i):
                act.wait_ge(scale_l_ready, i + 1)
                a.activation(x2f, x1b, ACT.Identity, scale=scale_l[:, :], bias=shift_l[:, :]).then_inc(norm_l, 1)

            def high_of_x2(i):
                act.wait_ge(norm_l, i + 1)
                act.wait_ge(x2_out, i * 16)
                a.activation(x2nat[:, 0, :], x2f, ACT.Copy).then_inc(x2_high, 1)

            def x_tile(b, j, u):
                if not isinstance(j, int) or j < BT - 1:
                    take_q(b, j + 1)
                if not isinstance(j, int) or j < BT - 2:
                    high_of_nat(b * (2 * BT) + j + (BT + 2), b * SETS + set_of_x(j + 1) + 1, u)
                if not isinstance(j, int) or j >= 0:
                    root_l(b * BT + j)
                if not isinstance(j, int) or j < BT - LEAD:
                    root_q(b * BT + j + LEAD, 1 - u)
                if not isinstance(j, int) or j >= 0:
                    normalise_l(b * BT + j)
                if not isinstance(j, int) or j < BT - LEAD:
                    normalise_q(b * BT + j + LEAD, 1 - u)
                if not isinstance(j, int) or j >= 0:
                    high_of_x2(b * BT + j)
                    take_x2(b, SETS - 1 if isinstance(j, int) and j == BT - 1 else set_of_x2(j))

            with act.Fori(0, B) as b:
                i0, n0 = b * BT, b * (2 * BT)
                high_of_nat(n0, b * SETS, 0)
                with act.Fori(0, BT // 2 - 1) as q:
                    for u in range(2):
                        high_of_nat(n0 + q * 2 + (u + 1), b * SETS + q * 2 + (u + 1), 1 - u)
                        take_ctx(b, q * 2 + u)
                high_of_nat(n0 + (BT - 1), b * SETS + (BT - 1), 1)
                take_ctx(b, BT - 2)
                root_q(i0, 0)
                root_q(i0 + 1, 1)
                normalise_q(i0, 0)
                normalise_q(i0 + 1, 1)
                take_ctx(b, BT - 1)
                high_of_nat(n0 + BT, b * SETS + BT, 0)
                x_tile(b, -1, 1)
                x_tile(b, 0, 0)
                with act.Fori(0, (BT - LEAD - 1) // 2) as q:
                    for u in range(2):
                        x_tile(b, q * 2 + (u + 1), 1 - u)
                for j in range(BT - LEAD, BT):
                    x_tile(b, j, j % 2)

            act.wait_ge(top_ready, 1)
            a.activation(top_w[:, :, :], top_w[:, :, :], ACT.Sigmoid, scale=1.0 / WSCALE).then_inc(sig_ready, 1)

            def load_x(n, row):
                act.dma_start(xin[:, :, :].rearrange("p a d -> p (a d)"), rows_x[ds(row, P), :]).then_inc(xin_in, 16)

            def take_xt(n):
                act.wait_ge(trx, n + 1)
                a.activation(xT[:, 0, :, :], ps_t[:, 0, :].rearrange("p (k n) -> p k n", k=KH), ACT.Copy)\
                    .then_inc(xt_high, 1)

            def silu(n):
                act.wait_ge(gu_done, n + 1)
                a.activation(sil[:, :, :], ps_gu[:, 0:2, 0:CH], ACT.Silu, scale=1.0 / WSCALE).then_inc(silu_done, 1)

            def high_of_hidden(n):
                act.wait_ge(hid_done, n + 1)
                a.activation(hid_hl[:, 0, :], hid[:, :, :].rearrange("p a c -> p (a c)"), ACT.Copy)\
                    .then_inc(hid_high, 1)

            def take_ht(n):
                act.wait_ge(trh, n + 1)
                a.activation(hT[:, 0, 0:KM * P], ps_t[:, 0, 0:KM * P], ACT.Copy).then_inc(ht_high, 1)

            def store_d(n, free=True):
                act.wait_ge(down_done, n + 1)
                if free:
                    act.wait_ge(d_out, n * 16)
                a.activation(dout[:, :], ps_d_flat, ACT.Copy, scale=1.0 / (WSCALE * HSCALE)).then_inc(d_free, 1)
                act.wait_ge(d_free, n + 2)
                act.dma_start(rows_d[ds(n * P, P), :], dout[:, :]).then_inc(d_out, 16)

            def tile(n, next_row=None, last=False, before="none"):
                silu(n)
                if not last:
                    take_xt(n + 1)
                if next_row is not None:
                    load_x(n + 2, next_row)
                high_of_hidden(n)
                if before != "none":
                    store_d(n - 1, before == "free")
                take_ht(n)

            act.wait_ge(x2_out, 16 * TT)
            act.wait_ge(routed, 1)
            load_x(0, 0)
            take_xt(0)
            load_x(1, P)
            tile(0, 2 * P)
            tile(1, 3 * P, before="fresh")
            with act.Fori(2, A_LAST) as n:
                tile(n, (n + 2) * P, before="free")
            act.wait_ge(pad_out, 16 * E)
            for u in range(2):
                act.wait_ge(scat_out[u], 16 * TOPK * TT // 2)
            with act.Fori(A_LAST, N_ALL - 2) as n:
                tile(n, (n + 2) * P, before="free")
            tile(N_ALL - 2, before="free")
            tile(N_ALL - 1, last=True, before="free")
            store_d(N_ALL - 1)

            n_tiles = act.value_load(count_tab[0:1, 0:1], min_val=N_ALL, max_val=N_B)
            with act.Fori(N_ALL, N_B) as n:
                with act.If(n < n_tiles):
                    load_x(n, n * P)
                    take_xt(n)
                    silu(n)
                    high_of_hidden(n)
                    take_ht(n)
                    store_d(n)
                with act.Else():
                    act.wait_ge(d_free, n + 1)
                    act.wait_ge(d_out, n * 16)
                    act.dma_start(rows_d[ds(n * P, P), :], dout[:, :]).then_inc(d_out, 16)
                    act.wait_ge(xin_in, n * 16)
                    act.sem_inc(xin_in, 16)
                    for done in (xt_high, silu_done, hid_high, ht_high, d_free):
                        act.sem_inc(done, 1)

            load_x(N_B, 0)
            take_xt(N_B)
            load_x(N_B + 1, P)
            with act.Fori(N_B, N_B + TT - 2) as n:
                tile(n, (n + 2 - N_B) * P)
            tile(N_B + TT - 2)
            tile(N_B + TT - 1, last=True)

        @block.vector
        def _(dve):
            v = nc.vector
            for free in (qin_free, x1_free, logits_free):
                dve.sem_inc(free, 1)

            def blocks(ap):
                return ap.rearrange("p (k n) -> p k n", k=KH)

            def per_block(ap):
                return ap.unsqueeze(2).to_broadcast([P, KH, P])

            step = Chain(dve, gw_step, 0)
            dve.wait_ge(gw_in, 16)
            step(v.tensor_scalar(gw_f[:, :], gw_f[:, :], WSCALE, None, ALU.mult))
            step(v.tensor_copy(gw[:, 0, :], gw_f[:, :]))
            v.tensor_tensor(gw[:, 1, :], gw_f[:, :], gw[:, 0, :], ALU.subtract).then_inc(gw_ready, 1)
            dve.wait_ge(const_ready, CONSTS)

            def guard(step, block_amax, eps, scale):
                step(v.tensor_scalar(safe[:, :], block_amax, eps, None, ALU.max))
                v.tensor_scalar(from_q[:, :], safe[:, :], 1.0 / FP8_MAX, scale, ALU.mult, ALU.mult)
                step(v.reciprocal(to_q[:, :], safe[:, :]))
                step(v.tensor_scalar(to_q[:, :], to_q[:, :], FP8_MAX, None, ALU.mult))

            def quantise(step, n, u):
                dve.wait_ge(nat_ready, n)
                v.tensor_tensor(blocks(deq[u]), blocks(qin[u]), per_block(to_q[:, :]), ALU.mult)\
                    .then_inc(qin_free, 1)
                dve.wait_ge(qin_free, n + 2)
                step(v.tensor_scalar(rnd.bitcast(I32), deq[u].bitcast(I32), EXP_MASK, None, ALU.bitwise_and))
                step(v.tensor_scalar(rnd, rnd, FP8_MIN_EXP, FP8_ROUND, ALU.max, ALU.mult))
                step(v.tensor_tensor(deq[u], deq[u], rnd, ALU.add))
                step(v.tensor_tensor(deq[u], deq[u], rnd, ALU.subtract))
                v.tensor_tensor(blocks(deq[u]), blocks(deq[u]), per_block(from_q[:, :]), ALU.mult)\
                    .then_inc(deq_ready, 1)

            def ctx_max(c, load, u):
                dve.wait_ge(qin_in[u], load * 16 + 16)
                v.tensor_reduce(amax_p[:, u, :], blocks(qin[u]), AX.X, ALU.max, apply_absolute_value=True)\
                    .then_inc(block_max, 1)

            def ctx_tile(c, n, u):
                step = Chain(dve, ctx_step, c * CTX_STEPS)
                dve.wait_ge(block_max_all, c + 1)
                guard(step, amax[:, u, :], W_EPS, WSCALE)
                quantise(step, n, u)
                assert step.n == CTX_STEPS

            def moments(step, src, stats, mv, var, ready):
                v.bn_stats(stats[:, 0:6], src[:, 0:512])
                step(v.bn_stats(stats[:, 6:12], src[:, 512:1024]))
                dve.sem_inc(dve_turn, 1)
                step(v.bn_aggr(mv, stats[:, :]))
                v.tensor_scalar(var, mv[:, 1:2], LN_EPS, None, ALU.add).then_inc(ready, 1)

            def x_moments(i, load, u):
                dve.wait_ge(qin_in[u], load * 16 + 16)
                moments(Chain(dve, mean_step, i * MEAN_STEPS), qin[u], stats_q, mv_q[:, 2 * u:2 * u + 2],
                        var_q[:, u:u + 1], var_q_ready)

            def x_scale(i, u):
                dve.wait_ge(std_q_ready, i + 1)
                v.reciprocal(scale_q[:, u:u + 1], std_q[:, u:u + 1]).then_inc(scale_step, 1)
                dve.wait_ge(scale_step, i + 1)
                v.tensor_scalar(shift_q[:, u:u + 1], mv_q[:, 2 * u:2 * u + 1], scale_q[:, u:u + 1], -1.0,
                                ALU.mult, ALU.mult).then_inc(scale_q_ready, 1)

            def x_tile(i, n, u):
                step = Chain(dve, x_step, i * X_STEPS)
                dve.wait_ge(norm_q, i + 1)
                step(v.tensor_reduce(amax[:, u, :], blocks(qin[u]), AX.X, ALU.max, apply_absolute_value=True))
                guard(step, amax[:, u, :], ACT_EPS, 1.0)
                quantise(step, n, u)
                assert step.n == X_STEPS

            def residual(i):
                step = Chain(dve, ln_step, i * LN_STEPS)
                dve.wait_ge(attn_done, i + 1)
                dve.wait_ge(xres_in, i * 16 + 16)
                dve.wait_ge(x1_out, i * 16)
                v.scalar_tensor_tensor(out=x1b, in0=ps_d_flat, scalar=1.0 / WSCALE, in1=xres, op0=ALU.mult,
                                       op1=ALU.add).then_inc(x1_free, 1)
                dve.wait_ge(x1_free, i + 2)
                moments(step, x1b, stats_l, mv_l[:, :], var_l[:, :], var_l_ready)

            def x2_scale(i):
                step = Chain(dve, ln_step, i * LN_STEPS + (LN_STEPS - 1))
                dve.wait_ge(std_l_ready, i + 1)
                step(v.reciprocal(scale_l[:, :], std_l[:, :]))
                v.tensor_scalar(shift_l[:, :], mv_l[:, 0:1], scale_l[:, :], -1.0, ALU.mult,
                                ALU.mult).then_inc(scale_l_ready, 1)

            def choose(i):
                step = Chain(dve, top_step, i * TOP_STEPS)
                dve.wait_ge(logits_done, i + 1)
                step(v.tensor_reduce(group8[:, 0:GROUPS], ps_logits.rearrange("p (g e) -> p g e", g=GROUPS), AX.X,
                                     ALU.max))
                dve.sem_inc(dve_turn, 1)
                step(v.max(group_top[:, :], group8[:, :]))
                dve.sem_inc(dve_turn, 1)
                step(v.max_index(group_idx[:, :], group_top[:, :], group8[:, :]))
                step(v.tensor_copy(group_f[:, :], group_idx[:, 0:TOPG]))
                step(v.tensor_scalar(chosen[:, :], iota_e[:, 0:GROUPS], group_f[:, 0:1], None, ALU.is_equal))
                step(v.scalar_tensor_tensor(out=chosen2[:, :], in0=iota_e[:, 0:GROUPS], scalar=group_f[:, 1:2],
                                            in1=chosen[:, :], op0=ALU.is_equal, op1=ALU.add))
                step(v.tensor_scalar(chosen[:, :], chosen2[:, :], -NEG, NEG, ALU.mult, ALU.add))
                v.tensor_tensor(masked[:, :].rearrange("p (g e) -> p g e", g=GROUPS),
                                ps_logits.rearrange("p (g e) -> p g e", g=GROUPS),
                                chosen[:, :].unsqueeze(2).to_broadcast([P, GROUPS, E // GROUPS]),
                                ALU.add).then_inc(logits_free, 1)
                dve.wait_ge(logits_free, i + 2)
                dve.sem_inc(dve_turn, 1)
                step(v.max(expert_top[:, :], masked[:, :]))
                dve.sem_inc(dve_turn, 1)
                step(v.max_index(expert_idx[:, :], expert_top[:, :], masked[:, :]))
                v.tensor_copy(top_w[:, ds(i, 1), :].rearrange("p a k -> p (a k)"), expert_top[:, 0:TOPK])
                step(v.tensor_copy(top_idx[:, ds(i, 1), :].rearrange("p a k -> p (a k)"), expert_idx[:, 0:TOPK]))
                assert step.n == TOP_STEPS

            def x_step_of(b, j, u, half):
                i, n = b * BT + j, b * (2 * BT) + j + BT
                ahead = not isinstance(j, int) or j < BT - LEAD
                residual(i)
                if ahead:
                    x_moments(i + LEAD, b * BT + half + BT // 2, 1 - u)
                x2_scale(i)
                if ahead:
                    x_scale(i + LEAD, 1 - u)
                if not isinstance(j, int) or j > 0:
                    choose(i - 1)
                if ahead:
                    x_tile(i + LEAD, n + LEAD, 1 - u)

            with dve.Fori(0, B) as b:
                i0, n0 = b * BT, b * (2 * BT)
                ctx_max(i0, i0, 0)
                with dve.Fori(0, BT // 2 - 1) as q:
                    for u in range(2):
                        ctx_max(i0 + q * 2 + (u + 1), i0 + q + u, 1 - u)
                        ctx_tile(i0 + q * 2 + u, n0 + q * 2 + u, u)
                ctx_max(i0 + (BT - 1), i0 + (BT // 2 - 1), 1)
                ctx_tile(i0 + (BT - 2), n0 + (BT - 2), 0)
                ctx_tile(i0 + (BT - 1), n0 + (BT - 1), 1)
                x_moments(i0, i0 + BT // 2, 0)
                x_moments(i0 + 1, i0 + BT // 2, 1)
                x_scale(i0, 0)
                x_scale(i0 + 1, 1)
                x_tile(i0, n0 + BT, 0)
                x_tile(i0 + 1, n0 + (BT + 1), 1)
                x_moments(i0 + 2, i0 + (BT // 2 + 1), 0)
                x_scale(i0 + 2, 0)
                x_tile(i0 + 2, n0 + (BT + 2), 0)
                x_step_of(b, 0, 0, LEAD // 2)
                with dve.Fori(0, (BT - LEAD - 1) // 2) as q:
                    for u in range(2):
                        x_step_of(b, q * 2 + (u + 1), 1 - u, q + (1 + LEAD) // 2)
                for j in range(BT - LEAD, BT):
                    x_step_of(b, j, j % 2, None)
                choose(i0 + (BT - 1))

            dve.sem_inc(top_ready, 1)
            dve.wait_ge(x1_out, 16 * TT)
            dve.wait_ge(x2_out, 16 * TT)
            step = Chain(dve, route_step, 0)
            full = [P, TT, TOPK, E]
            for k in range(TOPK):
                last = v.tensor_tensor(hot[:, :, k, :], top_idx[:, :, k:k + 1].to_broadcast([P, TT, E]),
                                       iota_e[:, :].unsqueeze(1).to_broadcast([P, TT, E]), ALU.is_equal)
            step(last)
            with nc.allow_low_precision(reason="at most one of the six is 1"):
                step(v.tensor_reduce(mask, hot.rearrange("p t k e -> p t e k"), AX.X, ALU.add))
            v.memset(pre_a[:, 0:1, :], 0.0)
            step(v.tensor_copy(pre_a[:, 1:TT, :], mask[:, 0:TT - 1, :]))
            src, dst, d = pre_a, pre_b, 1
            while d < TT:
                v.tensor_copy(dst[:, 0:d, :], src[:, 0:d, :])
                step(v.tensor_tensor(dst[:, d:TT, :], src[:, d:TT, :], src[:, 0:TT - d, :], ALU.add))
                src, dst, d = dst, src, 2 * d
            assert src is pre_b
            dve.sem_inc(mask_ready, 1)
            dve.wait_ge(sig_ready, 1)
            step(v.tensor_reduce(w_sum[:, :], top_w[:, :, :], AX.X, ALU.add))
            step(v.reciprocal(w_sum[:, :], w_sum[:, :]))
            step(v.tensor_tensor(top_w[:, :, :], top_w[:, :, :],
                                 w_sum[:, :].unsqueeze(2).to_broadcast([P, TT, TOPK]), ALU.mult))
            dve.wait_ge(rank_done, 1)
            step(v.tensor_copy(count[:, :], ps_gu[:, 2, 0:E]))
            step(v.tensor_scalar(tiles_e[:, :], count[:, :], P - 1.0, 1.0 / P, ALU.add, ALU.mult))
            step(v.tensor_scalar(tiles_e[:, :], tiles_e[:, :], -127.0 / 256, 2.0 ** 23, ALU.add, ALU.add))
            step(v.tensor_scalar(tiles_e[:, :], tiles_e[:, :], -2.0 ** 23, None, ALU.add))
            step(v.tensor_tensor_scan(ends[:, :], ones_f[:, :], tiles_e[:, :], 0.0, ALU.mult, ALU.add))
            step(v.tensor_tensor(first_slot[:, :], ends[:, :], tiles_e[:, :], ALU.subtract))
            step(v.tensor_scalar(first_slot[:, :], first_slot[:, :], float(P), float(T), ALU.mult, ALU.add))
            step(v.tensor_tensor(place, ps_gu[:, 0:2, :].rearrange("p a (t e) -> p (a t) e", e=E),
                                 first_slot[:, :].unsqueeze(1).to_broadcast([P, TT, E]), ALU.add))
            for k in range(TOPK):
                last = v.tensor_tensor(prod[:, :, k, :], hot[:, :, k, :], place, ALU.mult)
            step(last)
            step(v.tensor_reduce(top_idx[:, :, :], prod, AX.X, ALU.add))
            step(v.tensor_copy(slot[:, :, :], top_idx[:, :, :]))
            step(v.tensor_tensor(tab_cmp, iota_t[0:1, :].unsqueeze(2).to_broadcast([1, SLOT_TILES, E]),
                                 ends[0:1, :].unsqueeze(1).to_broadcast([1, SLOT_TILES, E]), ALU.is_ge))
            step(v.tensor_reduce(expert_t[0:1, :], tab_cmp, AX.X, ALU.add))
            v.memset(ready_tab[0:1, 0:TT], 1)
            v.memset(buf_tab[0:1, 0:TT], 0)
            v.memset(done_tab[0:1, 0:1], 1)
            v.memset(done_tab[0:1, 1:2], TT)
            v.tensor_scalar(done_tab[0:1, 2:E + 2], ends[0:1, :], float(TT), None, ALU.add)
            v.tensor_scalar(count_tab[0:1, :], ends[0:1, E - 1:E], float(TT), None, ALU.add)
            step(v.tensor_scalar(ready_tab[0:1, TT:], expert_t[0:1, :], E - 1.0, 2.0, ALU.min, ALU.add))
            step(v.tensor_scalar(buf_tab[0:1, TT:], ready_tab[0:1, TT:], 1, 1, ALU.bitwise_and, ALU.bitwise_xor))
            step(v.tensor_scalar(tmp_e[:, :], tiles_e[:, :], float(P), iota_p[:, :], ALU.mult, ALU.add))
            step(v.scalar_tensor_tensor(out=tmp_e[:, :], in0=tmp_e[:, :], scalar=-float(P), in1=count[:, :],
                                        op0=ALU.add, op1=ALU.is_ge))
            step(v.tensor_scalar(first_slot[:, :], ends[:, :], float(P), iota_p[:, :], ALU.mult, ALU.add))
            step(v.tensor_scalar(first_slot[:, :], first_slot[:, :], T - P + FAR, None, ALU.add))
            v.scalar_tensor_tensor(out=pad_idx[:, :], in0=tmp_e[:, :], scalar=-FAR, in1=first_slot[:, :],
                                   op0=ALU.mult, op1=ALU.add).then_inc(routed, 1)

            def take_xt(n):
                dve.wait_ge(trx, n + 1)
                v.tensor_copy(xT[:, 1, :, :].rearrange("p k n -> p (k n)"), ps_t[:, 1, :]).then_inc(xt_low, 1)

            def hidden(n):
                dve.wait_ge(silu_done, n + 1)
                v.scalar_tensor_tensor(out=hid[:, :, :], in0=ps_gu[:, 2:4, 0:CH], scalar=HSCALE / WSCALE,
                                       in1=sil[:, :, :], op0=ALU.mult, op1=ALU.mult).then_inc(hid_done, 1)

            def low_of_hidden(n):
                dve.wait_ge(hid_high, n + 1)
                v.tensor_tensor(hid_hl[:, 1, :], hid[:, :, :].rearrange("p a c -> p (a c)"), hid_hl[:, 0, :],
                                ALU.subtract).then_inc(hid_low, 1)

            def take_ht(n):
                dve.wait_ge(trh, n + 1)
                v.tensor_copy(hT[:, 1, 0:KM * P], ps_t[:, 1, 0:KM * P]).then_inc(ht_low, 1)

            def tile(n, last=False, before=None):
                hidden(n)
                if not last:
                    take_xt(n + 1)
                low_of_hidden(n)
                if before is not None:
                    combine(*before)
                take_ht(n)

            def combine(i, u, pair):
                step = Chain(dve, comb_step, i * COMB_STEPS)
                dve.wait_ge(down_done, i + (N_B + 1))
                dve.wait_ge(side_in[u], pair * 32 + 32)
                v.scalar_tensor_tensor(out=total[u], in0=ps_d_flat, scalar=1.0 / (WSCALE * HSCALE), in1=total[u],
                                       op0=ALU.mult, op1=ALU.add).then_inc(d_free, 1)
                dve.wait_ge(d_free, i + (N_B + 2))
                step(v.tensor_tensor(total[u], total[u], a_rows[u], ALU.add))
                dve.wait_ge(gat_in[u], pair * (16 * TOPK) + 16 * TOPK)
                for k in range(TOPK):
                    ins = v.scalar_tensor_tensor(
                        out=total[u], in0=gat[u][:, k, :],
                        scalar=top_w[:, ds(i, 1), k:k + 1].rearrange("p a k -> p (a k)"), in1=total[u],
                        op0=ALU.mult, op1=ALU.add)
                    if k < TOPK - 1:
                        step(ins)
                    else:
                        ins.then_inc(comb_done, 1)
                assert step.n == COMB_STEPS

            take_xt(0)
            with dve.Fori(0, N_ALL - 1) as n:
                tile(n)
            tile(N_ALL - 1, last=True)

            n_tiles = dve.value_load(count_tab[0:1, 0:1], min_val=N_ALL, max_val=N_B)
            with dve.Fori(N_ALL, N_B) as n:
                with dve.If(n < n_tiles):
                    take_xt(n)
                    hidden(n)
                    low_of_hidden(n)
                    take_ht(n)
                with dve.Else():
                    dve.wait_ge(ht_low, n)
                    for done in (xt_low, hid_done, hid_low, ht_low):
                        dve.sem_inc(done, 1)

            take_xt(N_B)
            tile(N_B)
            with dve.Fori(0, TT // 2 - 1) as q:
                tile(q * 2 + (N_B + 1), before=(q * 2, 0, q))
                tile(q * 2 + (N_B + 2), before=(q * 2 + 1, 1, q))
            tile(N_B + TT - 1, last=True, before=(TT - 2, 0, TT // 2 - 1))
            combine(TT - 1, 1, TT // 2 - 1)


_INS = ["x", "ctx_2048", "L0_ffn_gate_w", "L0_ffn_w_gate", "L0_ffn_w_up", "L0_ffn_w_down", "L0_ffn_sw_gate",
        "L0_ffn_sw_up", "L0_ffn_sw_down"]


def kernel(**inputs):
    import numpy as _np
    import concourse.bacc as _bacc
    from concourse.bass_utils import run_bass_kernel_spmd as _run

    nc = _bacc.Bacc("TRN2", target_bir_lowering=False, num_devices=1)
    arrays, args = {}, []
    for name in _INS:
        a = _np.ascontiguousarray(inputs[name])
        arrays[f"in_{name}"] = a
        args.append(nc.dram_tensor(f"in_{name}", a.shape, mybir.dt.from_np(a.dtype), kind="ExternalInput").ap())
    out = nc.dram_tensor("out_0", (B, S, H), F32, kind="ExternalOutput").ap()
    build(nc, *args, out)
    r = _run(nc, [arrays], core_ids=[0])
    return r.results[0]["out_0"]
```

```python
from contextlib import ExitStack

import concourse.bass as bass
from concourse import mybir

F32 = mybir.dt.float32
F16 = mybir.dt.float16
I32 = mybir.dt.int32
U32 = mybir.dt.uint32
ALU = mybir.AluOpType
ACT = mybir.ActivationFunctionType
AX = mybir.AxisListType
ds = bass.ds

P = 128
B, S, H = 4, 1024, 1024
E, TOPK, GROUPS, TOPG = 32, 6, 4, 2
M = 704
KH = H // P
KM = -(-M // P)
M_LAST = M - (KM - 1) * P
T = B * S
TT = T // P
BT = S // P
CH = M // 2
FULL = T * TOPK // P
EXTRA = E - 1
SLOT_TILES = FULL + EXTRA
K_LAST = (KM - 1) * P
assert M_LAST * 2 == P
GU = KH * 2 * M
WCOLS = GU + KM * H
CHUNKS = KH + KM
STAGES = 4
BUF_UNIT = 64

FP8_MAX, ACT_EPS, W_EPS, LN_EPS = 448.0, 1e-4, 1e-6, 1e-5
EXP_MASK = 0x7F800000
FP8_MIN_EXP = 2.0 ** -6
FP8_ROUND = 1.5 * 2.0 ** 20
WSCALE = 256.0
HSCALE = 16.0
FAR = 2.0 ** 20
NEG = -1.0e30



class Chain:

    def __init__(self, engine, sem, base):
        self.engine, self.sem, self.base, self.n = engine, sem, base, 0

    def __call__(self, instruction):
        self.n += 1
        instruction.then_inc(self.sem, 1)
        self.engine.wait_ge(self.sem, self.base + self.n)


def build(nc, x, ctx_in, gate_w, w_gate, w_up, w_down, sw_gate, sw_up, sw_down, out):
    x_rows = x.rearrange("b s d -> (b s) d")
    c_rows = ctx_in.rearrange("b s d -> (b s) d")
    o_rows = out.rearrange("b s d -> (b s) d")

    rows_x = nc.dram_tensor("rows_x", (T + SLOT_TILES * P, 2 * H), F16).ap()
    rows_d = nc.dram_tensor("rows_d", (T + SLOT_TILES * P, H), F32).ap()
    rows_x1 = nc.dram_tensor("rows_x1", (T, H), F32).ap()
    last_row = T + SLOT_TILES * P - 1

    with ExitStack() as stack:
        def sb(name, shape, dt):
            return stack.enter_context(nc.sbuf_tensor(name, shape, dt))

        def psum(name, shape, dt):
            return stack.enter_context(nc.psum_tensor(name, shape, dt))

        def sem(name):
            return stack.enter_context(nc.semaphore(name))

        wts = sb("wts", [P, 2, 2, WCOLS], F16)
        stage = sb("stage", [P, STAGES, 2 * M], F32)
        xin = sb("xin", [P, 2, H], F16)
        xT = sb("xT", [P, 2, KH, P], F16)
        sil = sb("sil", [P, 2, CH], F32)
        hid = sb("hid", [P, 2, CH], F32)
        hid_hl = sb("hid_hl", [P, 2 * M], F16)
        hT = sb("hT", [P, 2, H], F16)
        dout = sb("dout", [P, H], F32)
        ident = sb("ident", [P, P], F16)
        upper = sb("upper", [P, P], F16)
        ones = sb("ones", [P, P], F16)
        ones_f = sb("ones_f", [P, E], F32)
        gw_f = sb("gw_f", [P, KH * E], F32)
        gw = sb("gw", [P, 2, KH * E], F16)
        iota_e = sb("iota_e", [P, E], F32)
        iota_p = sb("iota_p", [P, 1], F32)
        iota_t = sb("iota_t", [P, SLOT_TILES], F32)
        amax_p, amax = (sb(n, [P, 2, KH], F32) for n in ("amax_p", "amax"))
        safe, to_q, from_q = (sb(n, [P, KH], F32) for n in ("safe", "to_q", "from_q"))
        stats_q, mv_q, stats_l, mv_l = (sb(n, [P, w], F32) for n, w in (
            ("stats_q", 12), ("mv_q", 4), ("stats_l", 12), ("mv_l", 2)))
        var_q, std_q, scale_q, shift_q = (sb(n, [P, 2], F32) for n in ("var_q", "std_q", "scale_q", "shift_q"))
        var_l, std_l, scale_l, shift_l = (sb(n, [P, 1], F32) for n in ("var_l", "std_l", "scale_l", "shift_l"))
        group8, group_top, expert_top = (sb(n, [P, 8], F32) for n in ("group8", "group_top", "expert_top"))
        group_idx, expert_idx = sb("group_idx", [P, 8], U32), sb("expert_idx", [P, 8], U32)
        group_f = sb("group_f", [P, TOPG], F32)
        chosen, chosen2 = sb("chosen", [P, GROUPS], F32), sb("chosen2", [P, GROUPS], F32)
        masked = sb("masked", [P, E], F32)
        top_idx = sb("top_idx", [P, TT, TOPK], F32)
        top_w = sb("top_w", [P, TT, TOPK], F32)
        w_sum = sb("w_sum", [P, TT], F32)
        slot = sb("slot", [P, TT, TOPK], I32)
        count = sb("count", [P, E], F32)
        tiles_e, ends, first_slot, tmp_e = (sb(n, [P, E], F32) for n in ("tiles_e", "ends", "first_slot", "tmp_e"))
        expert_t = sb("expert_t", [1, SLOT_TILES], F32)
        ready_tab = sb("ready_tab", [1, TT + SLOT_TILES], I32)
        buf_tab = sb("buf_tab", [1, TT + SLOT_TILES], I32)
        tile_tab = sb("tile_tab", [1, TT + SLOT_TILES + 1], I32)
        row_tab = sb("row_tab", [1, EXTRA + 2], I32)
        count_f = sb("count_f", [1, 1], F32)
        row_n, row_wrap = sb("row_n", [1, EXTRA + 2], F32), sb("row_wrap", [1, EXTRA + 2], F32)
        done_tab = sb("done_tab", [1, E + 2], I32)
        count_tab = sb("count_tab", [1, 1], I32)
        pad_idx = sb("pad_idx", [P, E], I32)
        pad_now = sb("pad_now", [P, 4], I32)
        slot_now = sb("slot_now", [P, 2, TOPK], I32)

        early = wts[:, 1, :, :].rearrange("p a c -> p (a c)")
        cT = early[:, 0:2 * KH * S].rearrange("p (a k n) -> p a k n", a=2, k=KH)
        xqT = xin[:, :, :].rearrange("p a (k n) -> p a k n", k=KH)
        e0 = 2 * KH * S
        qin0, qin1, xres, x1b, deq0, deq1, rnd = (
            early[:, e0 + 2 * H * i:e0 + 2 * H * (i + 1)].bitcast(F32) for i in range(7))
        qin, deq = (qin0, qin1), (deq0, deq1)
        nat = early[:, e0 + 2 * H * 7:e0 + 2 * H * 8].rearrange("p (a d) -> p a d", a=2)
        x2nat = early[:, e0 + 2 * H * 8:e0 + 2 * H * 9].rearrange("p (a d) -> p a d", a=2)
        x2f = dout[:, :]
        n_hot = 2 * TT * TOPK * E
        hot, prod = (early[:, i * n_hot:(i + 1) * n_hot].bitcast(F32).rearrange("p (t k e) -> p t k e", t=TT, k=TOPK)
                     for i in range(2))
        mask, pre_a, pre_b = (early[:, 2 * n_hot + TT * E * i:2 * n_hot + TT * E * (i + 1)]
                              .rearrange("p (t e) -> p t e", t=TT) for i in range(3))
        place = early[:, 2 * n_hot + TT * E * 3:2 * n_hot + TT * E * 5].bitcast(F32).rearrange("p (t e) -> p t e", t=TT)
        tab_cmp = early[0:1, 0:2 * SLOT_TILES * E].bitcast(F32).rearrange("p (t e) -> p t e", t=SLOT_TILES)
        xsc = [early[:, 2 * H * i:2 * H * (i + 1)] for i in range(2)]
        zeros = early[:, 4 * H:6 * H]
        late = wts[:, 0, :, :].rearrange("p a c -> p (a c)").bitcast(F32)
        gat = [late[:, u * TOPK * H:(u + 1) * TOPK * H].rearrange("p (k d) -> p k d", k=TOPK) for u in range(2)]
        total = [late[:, (2 * TOPK + u) * H:(2 * TOPK + u + 1) * H] for u in range(2)]
        a_rows = [late[:, (2 * TOPK + 2 + u) * H:(2 * TOPK + 3 + u) * H] for u in range(2)]

        ps_t = psum("ps_t", [P, 2, H], F16)
        ps_gu = psum("ps_gu", [P, 4, 512], F32)
        ps_d = psum("ps_d", [P, 2, 512], F32)
        ps_d_flat = ps_d[:, :, :].rearrange("p a n -> p (a n)")
        ps_logits = ps_gu[:, 0, 0:E]

        const_ready, pool_step, gw_in, gw_step, gw_ready = (sem(n) for n in (
            "const_ready", "pool_step", "gw_in", "gw_step", "gw_ready"))
        conv_step, conv_done, weights_ready = (sem(n) for n in ("conv_step", "conv_done", "weights_ready"))
        qin_in = [sem(f"qin_in{u}") for u in range(2)]
        qin_free, xres_in, block_max, block_max_all = (sem(n) for n in (
            "qin_free", "xres_in", "block_max", "block_max_all"))
        var_q_ready, std_q_ready, scale_q_ready, norm_q = (sem(n) for n in (
            "var_q_ready", "std_q_ready", "scale_q_ready", "norm_q"))
        var_l_ready, std_l_ready, scale_l_ready, norm_l = (sem(n) for n in (
            "var_l_ready", "std_l_ready", "scale_l_ready", "norm_l"))
        deq_ready, nat_high, nat_ready, x1_free, x2_high, x2_ready = (sem(n) for n in (
            "deq_ready", "nat_high", "nat_ready", "x1_free", "x2_high", "x2_ready"))
        tr_done, tr_free, attn_done, logits_done, logits_free, x1_out, x2_out = (sem(n) for n in (
            "tr_done", "tr_free", "attn_done", "logits_done", "logits_free", "x1_out", "x2_out"))
        ctx_step, mean_step, scale_step, x_step, ln_step, top_step = (sem(n) for n in (
            "ctx_step", "mean_step", "scale_step", "x_step", "ln_step", "top_step"))
        route_step, top_ready, sig_ready, mask_ready, rank_done, routed, pad_out = (sem(n) for n in (
            "route_step", "top_ready", "sig_ready", "mask_ready", "rank_done", "routed", "pad_out"))
        xin_in, trx, xt_high, xt_low, gu_done, silu_done = (sem(n) for n in (
            "xin_in", "trx", "xt_high", "xt_low", "gu_done", "silu_done"))
        hid_done, hid_high, hid_low, trh, ht_high, ht_low, down_done, d_free, d_out = (sem(n) for n in (
            "hid_done", "hid_high", "hid_low", "trh", "ht_high", "ht_low", "down_done", "d_free", "d_out"))
        pe_turn, dve_turn, pool_turn = (sem(n) for n in ("pe_turn", "dve_turn", "pool_turn"))
        comb_step, comb_done, o_out = (sem(n) for n in ("comb_step", "comb_done", "o_out"))
        zeros_ready, zeros_out = sem("zeros_ready"), sem("zeros_out")
        stage_in = [sem(f"stage_in{i}") for i in range(STAGES)]
        xsc_in = [sem(f"xsc_in{u}") for u in range(2)]
        scat_out = [sem(f"scat_out{u}") for u in range(2)]
        gat_in = [sem(f"gat_in{u}") for u in range(2)]
        side_in = [sem(f"side_in{u}") for u in range(2)]

        CONSTS = 10
        SETS = 3 * BT
        LEAD = 3
        N_ALL = TT + FULL
        N_MAX = TT + SLOT_TILES
        A_LAST = TT - 2
        CTX_STEPS, MEAN_STEPS, X_STEPS, LN_STEPS, TOP_STEPS, COMB_STEPS = 7, 2, 8, 3, 10, 6

        def stage_of(o, c):
            return (o * CHUNKS + c) % STAGES

        def loads_of(o, c):
            return sum((g % STAGES) == stage_of(o, c) for g in range(o * CHUNKS + c + 1))

        def set_of_x(j):
            return BT if isinstance(j, int) and j == 0 else j * 2 + (BT - 1)

        def set_of_x2(j):
            return j * 2 + (BT + 2)

        pair_loads = [sum(g % STAGES == st for g in range(2 * CHUNKS)) for st in range(STAGES)]

        block = stack.enter_context(nc.Block())

        @block.sync
        def _(sp):
            def load_piece(o, c, gate, up, down):
                st = stage_of(o, c)
                if c < KH:
                    sp.dma_start(stage[:, st, 0:M], gate[c * P:(c + 1) * P, :]).then_inc(stage_in[st], 16)
                    sp.dma_start(stage[:, st, M:2 * M], up[c * P:(c + 1) * P, :]).then_inc(stage_in[st], 16)
                else:
                    r0 = (c - KH) * P
                    for h in range(2):
                        if c < CHUNKS - 1:
                            to, source = stage[:, st, h * 512:(h + 1) * 512], down[r0:r0 + P, h * 512:(h + 1) * 512]
                        else:
                            to, source = stage[h * M_LAST:(h + 1) * M_LAST, st, 0:H], down[r0:M, :]
                        sp.dma_start(to, source).then_inc(stage_in[st], 16)

            half_a = (sw_gate[:, 0:M], sw_up[:, 0:M], sw_down[0:M, :])
            half_b = (sw_gate[:, M:2 * M], sw_up[:, M:2 * M], sw_down[M:2 * M, :])
            sp.dma_start(gw_f[:, :].rearrange("p (k e) -> p k e", k=KH),
                         gate_w.rearrange("(k p) e -> p k e", p=P)).then_inc(gw_in, 16)
            for c in range(STAGES):
                load_piece(0, c, *half_a)

            def load_q(rows, row, n, u):
                sp.wait_ge(qin_free, n + 1)
                sp.dma_start(qin[u], rows[ds(row, P), :]).then_inc(qin_in[u], 16)

            def load_res(i):
                sp.wait_ge(x1_free, i + 1)
                sp.dma_start(xres, x_rows[ds(i * P, P), :]).then_inc(xres_in, 16)

            def store_x1(i):
                sp.wait_ge(x1_free, i + 2)
                sp.dma_start(rows_x1[ds(i * P, P), :], x1b).then_inc(x1_out, 16)

            def store_x2(i):
                sp.wait_ge(x2_ready, i + 1)
                sp.dma_start(rows_x[ds(i * P, P), :], x2nat.rearrange("p a d -> p (a d)")).then_inc(x2_out, 16)

            with sp.Fori(0, B) as b:
                i0, n0 = b * BT, b * (2 * BT)
                with sp.Fori(0, BT // 2) as q:
                    for u in range(2):
                        load_q(c_rows, (i0 + q * 2 + u) * P, n0 + q * 2 + u, u)
                for j in range(LEAD + 2):
                    load_q(x_rows, (i0 + j) * P, n0 + (BT + j), j % 2)
                    if j == 0:
                        load_res(i0)
                for j in range(BT - LEAD - 2):
                    store_x1(i0 + j)
                    load_res(i0 + (j + 1))
                    load_q(x_rows, (i0 + (j + LEAD + 2)) * P, n0 + (BT + j + LEAD + 2), (j + LEAD) % 2)
                    store_x2(i0 + j)
                with sp.Fori(BT - LEAD - 2, BT - 1) as j:
                    store_x1(i0 + j)
                    load_res(i0 + j + 1)
                    store_x2(i0 + j)
                store_x1(i0 + (BT - 1))
                store_x2(i0 + (BT - 1))

            for c in range(STAGES, CHUNKS):
                sp.wait_ge(conv_done, c - STAGES + 1)
                load_piece(0, c, *half_a)

            sp.wait_ge(routed, 1)
            for u in range(2):
                sp.dma_start(xsc[u], rows_x[u * P:(u + 1) * P, :]).then_inc(xsc_in[u], 16)
            sp.wait_ge(zeros_ready, 1)
            sp.dma_start(rows_d[T + FULL * P:, :].rearrange("(t p) d -> p t d", p=P),
                         zeros.bitcast(F32).unsqueeze(1).to_broadcast([P, EXTRA, H])).then_inc(zeros_out, 16)
            with sp.Fori(1, TT // 2) as q:
                for u in range(2):
                    sp.wait_ge(scat_out[u], q * (16 * TOPK))
                    sp.dma_start(xsc[u], rows_x[ds((q * 2 + u) * P, P), :]).then_inc(xsc_in[u], 16)

            with sp.Fori(0, E // 2) as q:
                for u in range(2):
                    mats = [w[ds(q * 2 + u, 1)].rearrange("a r c -> (a r) c") for w in (w_gate, w_up, w_down)]
                    for c in range(CHUNKS):
                        sp.wait_ge(conv_done, q * (2 * CHUNKS) + ((1 + u) * CHUNKS + c - STAGES + 1))
                        load_piece(1 + u, c, *mats)
            for c in range(CHUNKS):
                sp.wait_ge(conv_done, (E + 1) * CHUNKS + c - STAGES + 1)
                load_piece(1, c, *half_b)

            n_tiles = sp.value_load(count_tab[0:1, 0:1], min_val=N_ALL, max_val=N_MAX)
            sp.wait_ge(down_done, n_tiles)
            sp.wait_ge(d_out, n_tiles * 16 + 16)

            def side(i, u):
                sp.dma_start(total[u], rows_x1[ds(i * P, P), :]).then_inc(side_in[u], 16)
                sp.dma_start(a_rows[u], rows_d[ds(i * P, P), :]).then_inc(side_in[u], 16)

            def store_out(i, u):
                sp.wait_ge(comb_done, i + 1)
                sp.dma_start(o_rows[ds(i * P, P), :], total[u]).then_inc(o_out, 16)

            side(0, 0)
            side(1, 1)
            with sp.Fori(0, TT // 2 - 1) as q:
                for u in range(2):
                    store_out(q * 2 + u, u)
                    sp.wait_ge(o_out, q * 32 + 16 * (u + 1))
                    side(q * 2 + u + 2, u)
            store_out(TT - 2, 0)
            store_out(TT - 1, 1)
            sp.wait_ge(o_out, 16 * TT)

        @block.gpsimd
        def _(pool):
            g = nc.gpsimd
            g.memset(ident[:, :], 0.0).then_inc(pool_step, 1)
            g.memset(upper[:, :], 1.0).then_inc(pool_step, 1)
            g.memset(ones[:, :], 1.0).then_inc(const_ready, 1)
            g.memset(ones_f[:, :], 1.0).then_inc(const_ready, 1)
            g.memset(group8[:, :], -3.0e38).then_inc(const_ready, 1)
            pool.wait_ge(pool_step, 2)
            g.affine_select(out=ident[:, :], in_=ident[:, :], compare_op=ALU.not_equal, fill=1.0, base=0,
                            pattern=[[-1, P]], channel_multiplier=1).then_inc(const_ready, 1)
            g.affine_select(out=upper[:, :], in_=upper[:, :], compare_op=ALU.is_gt, fill=0.0, base=0,
                            pattern=[[1, P]], channel_multiplier=-1).then_inc(const_ready, 1)
            g.iota(iota_e[:, :], pattern=[[1, E]], base=0, channel_multiplier=0,
                   allow_small_or_imprecise_dtypes=True).then_inc(const_ready, 1)
            g.iota(iota_p[:, :], pattern=[[0, 1]], base=0, channel_multiplier=1,
                   allow_small_or_imprecise_dtypes=True).then_inc(const_ready, 1)
            g.iota(iota_t[:, :], pattern=[[1, SLOT_TILES]], base=0, channel_multiplier=0,
                   allow_small_or_imprecise_dtypes=True).then_inc(const_ready, 1)
            g.iota(row_n[:, :], pattern=[[1, EXTRA + 2]], base=N_ALL, channel_multiplier=0,
                   allow_small_or_imprecise_dtypes=True).then_inc(const_ready, 1)
            g.memset(amax[:, :, :], 0.0).then_inc(const_ready, 1)
            pool.sem_inc(nat_ready, 2)

            def split_piece(o, c, buf, pair=0):
                st = stage_of(o, c)
                cols, at = (2 * M, c * 2 * M) if c < KH else (H, GU + (c - KH) * H)
                high, low = wts[:, buf, 0, at:at + cols], wts[:, buf, 1, at:at + cols]
                raw = stage[:, st, 0:cols]
                step = pair * (4 * CHUNKS) + 2 * (o * CHUNKS + c)
                pool.wait_ge(stage_in[st], pair * (32 * pair_loads[st]) + 32 * loads_of(o, c))
                pool.sem_inc(pool_turn, 1)
                g.tensor_scalar(high, raw, WSCALE, 1.0, ALU.mult, ALU.mult).then_inc(conv_step, 1)
                g.tensor_scalar(raw, raw, WSCALE, 1.0, ALU.mult, ALU.mult).then_inc(conv_step, 1)
                pool.wait_ge(conv_step, step + 2)
                g.tensor_tensor(low, raw, high, ALU.subtract).then_inc(conv_done, 1)

            for c in range(STAGES):
                split_piece(0, c, 0)

            def all_max(c, u):
                pool.wait_ge(block_max, c + 1)
                pool.sem_inc(pool_turn, 1)
                g.partition_all_reduce(amax[:, u, :], amax_p[:, u, :], P,
                                       bass.bass_isa.ReduceOp.max).then_inc(block_max_all, 1)

            def low_of_nat(n, u):
                pool.wait_ge(nat_high, n + 1)
                g.tensor_tensor(nat[:, 1, :], deq[u], nat[:, 0, :], ALU.subtract).then_inc(nat_ready, 1)

            def low_of_x2(i):
                pool.wait_ge(x2_high, i + 1)
                g.tensor_tensor(x2nat[:, 1, :], x2f, x2nat[:, 0, :], ALU.subtract).then_inc(x2_ready, 1)

            with pool.Fori(0, B) as b:
                i0, n0 = b * BT, b * (2 * BT)
                all_max(i0, 0)
                with pool.Fori(0, BT // 2 - 1) as q:
                    for u in range(2):
                        all_max(i0 + q * 2 + (u + 1), 1 - u)
                        low_of_nat(n0 + q * 2 + u, u)
                all_max(i0 + (BT - 1), 1)
                for c in range(BT - 2, BT + LEAD - 1):
                    low_of_nat(n0 + c, c % 2)
                with pool.Fori(0, (BT - LEAD + 1) // 2) as q:
                    for u in range(2):
                        low_of_nat(n0 + q * 2 + (BT + LEAD - 1 + u), u)
                        low_of_x2(i0 + q * 2 + u)
                with pool.Fori(BT - LEAD + 1, BT) as j:
                    low_of_x2(i0 + j)
            for c in range(STAGES, CHUNKS):
                split_piece(0, c, 0)
            pool.wait_ge(conv_done, CHUNKS)
            pool.sem_inc(weights_ready, 1)

            pool.wait_ge(routed, 1)
            g.memset(zeros, 0.0).then_inc(pool_step, 1)
            pool.wait_ge(pool_step, 3)
            pool.sem_inc(zeros_ready, 1)

            def pad_four(q):
                g.tensor_copy(pad_now[:, :], pad_idx[:, ds(q * 4, 4)]).then_inc(pool_step, 1)
                pool.wait_ge(pool_step, q + 4)
                pool.sem_inc(pool_turn, 1)
                for u in range(4):
                    g.indirect_dma_start(
                        out=rows_x, out_offset=bass.IndirectOffsetOnAxis(ap=pad_now[:, u:u + 1], axis=0),
                        in_=zeros, in_offset=None, bounds_check=last_row, oob_is_err=False).then_inc(pad_out, 16)

            pad_four(0)
            with pool.Fori(1, E // 4) as q:
                pool.wait_ge(pad_out, q * 64)
                pad_four(q)

            with pool.Fori(0, TT // 2) as q:
                for u in range(2):
                    pool.wait_ge(xsc_in[u], q * 16 + 16)
                    g.tensor_copy(slot_now[:, u, :], slot[:, ds(q * 2 + u, 1), :].rearrange("p a k -> p (a k)")
                                  ).then_inc(pool_step, 1)
                    pool.wait_ge(pool_step, q * 2 + (u + 4 + E // 4))
                    pool.sem_inc(pool_turn, 1)
                    for k in range(TOPK):
                        g.indirect_dma_start(
                            out=rows_x, out_offset=bass.IndirectOffsetOnAxis(ap=slot_now[:, u, k:k + 1], axis=0),
                            in_=xsc[u], in_offset=None, bounds_check=last_row,
                            oob_is_err=False).then_inc(scat_out[u], 16)
            pool.wait_ge(zeros_out, 16)
            pool.wait_ge(pad_out, 16 * E)
            for u in range(2):
                pool.wait_ge(scat_out[u], 16 * TOPK * TT // 2)

            with pool.Fori(0, E // 2) as q:
                for u in range(2):
                    done = pool.value_load(done_tab[0:1, ds(q * 2 + u, 1)], min_val=1, max_val=N_MAX)
                    pool.wait_ge(down_done, done)
                    pool.sem_inc(pool_turn, 1)
                    for c in range(CHUNKS):
                        split_piece(1 + u, c, 1 - u, q)
                    pool.wait_ge(conv_done, q * (2 * CHUNKS) + (2 + u) * CHUNKS)
                    pool.sem_inc(weights_ready, 1)
            done = pool.value_load(done_tab[0:1, E:E + 1], min_val=1, max_val=N_MAX)
            pool.wait_ge(down_done, done)
            pool.sem_inc(pool_turn, 1)
            for c in range(CHUNKS):
                split_piece(1, c, 1, E // 2)
            pool.wait_ge(conv_done, (E + 2) * CHUNKS)
            pool.sem_inc(weights_ready, 1)

            n_tiles = pool.value_load(count_tab[0:1, 0:1], min_val=N_ALL, max_val=N_MAX)
            pool.wait_ge(down_done, n_tiles)
            pool.wait_ge(d_out, n_tiles * 16 + 16)
            pool.sem_inc(pool_turn, 1)

            def gather(i, u, step):
                g.tensor_copy(slot_now[:, u, :], slot[:, ds(i, 1), :].rearrange("p a k -> p (a k)")
                              ).then_inc(pool_step, 1)
                pool.wait_ge(pool_step, step)
                pool.sem_inc(pool_turn, 1)
                for k in range(TOPK):
                    g.indirect_dma_start(
                        out=gat[u][:, k, :], out_offset=None, in_=rows_d,
                        in_offset=bass.IndirectOffsetOnAxis(ap=slot_now[:, u, k:k + 1], axis=0),
                        bounds_check=last_row, oob_is_err=False).then_inc(gat_in[u], 16)

            step0 = 3 + E // 4 + TT
            gather(0, 0, step0 + 1)
            gather(1, 1, step0 + 2)
            with pool.Fori(1, TT // 2) as q:
                for u in range(2):
                    pool.wait_ge(comb_done, q * 2 + (u - 1))
                    gather(q * 2 + u, u, q * 2 + (u + 1 + step0))

        @block.tensor
        def _(pe):
            def transposes(src):
                for a in range(2):
                    for k in range(KH):
                        last = nc.tensor.transpose(ps_t[:, a, k * P:(k + 1) * P], src[:, a, k * P:(k + 1) * P],
                                                   ident[:, :])
                return last

            def three(dst, high, low, w_high, w_low, first, last):
                n = len(dst)
                for a, (left, right) in enumerate(((high, w_high), (high, w_low), (low, w_high))):
                    for c in range(n):
                        ins = nc.tensor.matmul(dst[c], left, right[c], start=(first and a == 0),
                                               stop=(last and a == 2))
                return ins

            pe.wait_ge(const_ready, CONSTS)
            pe.wait_ge(gw_ready, 1)
            pe.sem_inc(tr_done, 1)

            def tr(src, t, ready, n):
                pe.wait_ge(ready, n)
                pe.wait_ge(tr_free, t + 1)
                transposes(src).then_inc(tr_done, 1)

            def tr_ctx(b, j):
                tr(nat, b * SETS + j, nat_ready, b * (2 * BT) + j + 3)

            def tr_q(b, j):
                tr(nat, b * SETS + set_of_x(j), nat_ready, b * (2 * BT) + j + (BT + 3))

            def tr_x2(b, j, t):
                tr(x2nat, b * SETS + t, x2_ready, b * BT + j + 1)

            def attend(b, j, x2_too):
                pe.wait_ge(tr_free, b * SETS + set_of_x(j) + 2)
                pe.wait_ge(x1_free, b * BT + j + 1)
                for k in range(KH):
                    if x2_too and k == KH - 2:
                        tr_x2(b, j - 1, set_of_x2(j - 1))
                    ins = three([ps_d[:, c, :] for c in range(2)], xqT[:, 0, k, :], xqT[:, 1, k, :],
                                [cT[:, 0, k, c * 512:(c + 1) * 512] for c in range(2)],
                                [cT[:, 1, k, c * 512:(c + 1) * 512] for c in range(2)], k == 0, k == KH - 1)
                ins.then_inc(attn_done, 1)

            def logits(b, j, t):
                pe.wait_ge(tr_free, b * SETS + t + 2)
                pe.wait_ge(logits_free, b * BT + j + 1)
                for k in range(KH):
                    ins = three([ps_logits], xT[:, 0, k, :], xT[:, 1, k, :], [gw[:, 0, k * E:(k + 1) * E]],
                                [gw[:, 1, k * E:(k + 1) * E]], k == 0, k == KH - 1)
                ins.then_inc(logits_done, 1)

            with pe.Fori(0, B) as b:
                with pe.Fori(0, BT) as j:
                    tr_ctx(b, j)
                tr_q(b, 0)
                attend(b, 0, False)
                tr_q(b, 1)
                with pe.Fori(1, BT - 1) as j:
                    attend(b, j, True)
                    tr_q(b, j + 1)
                    logits(b, j - 1, set_of_x2(j - 1))
                attend(b, BT - 1, True)
                logits(b, BT - 2, set_of_x2(BT - 2))
                tr_x2(b, BT - 1, SETS - 1)
                logits(b, BT - 1, SETS - 1)

            pe.wait_ge(mask_ready, 1)
            half = TT // 2
            for c in range(2):
                nc.tensor.matmul(ps_gu[:, c, :], upper[:, :],
                                 mask[:, c * half:(c + 1) * half, :].rearrange("p t e -> p (t e)"),
                                 start=True, stop=False)
                nc.tensor.matmul(ps_gu[:, c, :], ones[:, :],
                                 pre_b[:, c * half:(c + 1) * half, :].rearrange("p t e -> p (t e)"),
                                 start=False, stop=True)
            nc.tensor.matmul(ps_gu[:, 2, 0:E], ones[:, :], mask[:, TT - 1, :], start=True, stop=False)
            nc.tensor.matmul(ps_gu[:, 2, 0:E], ones[:, :], pre_b[:, TT - 1, :], start=False,
                             stop=True).then_inc(rank_done, 1)
            pe.wait_ge(routed, 1)

            def tr_x(n):
                pe.wait_ge(xin_in, n * 16 + 16)
                transposes(xin).then_inc(trx, 1)

            def gate_up(n, buf):
                for k in range(KH):
                    cols = [k * 2 * M + c * CH for c in range(4)]
                    ins = three([ps_gu[:, c, 0:CH] for c in range(4)], xT[:, 0, k, :], xT[:, 1, k, :],
                                [wts[:, buf, 0, a:a + CH] for a in cols],
                                [wts[:, buf, 1, a:a + CH] for a in cols], k == 0, k == KH - 1)
                ins.then_inc(gu_done, 1)

            def tr_h(n):
                pe.wait_ge(hid_high, n + 1)
                pe.wait_ge(hid_low, n + 1)
                for a, blocks in ((0, KM), (1, KM - 1)):
                    for k in range(blocks):
                        at = a * KM * P + k * P
                        last = nc.tensor.transpose(ps_t[:, a, k * P:(k + 1) * P], hid_hl[:, at:at + P], ident[:, :])
                last.then_inc(trh, 1)

            def down(n, buf):
                outs = [ps_d[:, c, :] for c in range(2)]

                def weights(half, k, rows=P):
                    at = GU + k * H
                    return [wts[0:rows, buf, half, at + c * 512:at + (c + 1) * 512] for c in range(2)]

                for k in range(KM - 1):
                    three(outs, hT[:, 0, k * P:(k + 1) * P], hT[:, 1, k * P:(k + 1) * P], weights(0, k),
                          weights(1, k), k == 0, False)
                for c in range(2):
                    nc.tensor.matmul(outs[c], hT[:, 0, K_LAST:KM * P], weights(0, KM - 1)[c], start=False, stop=False)
                for c in range(2):
                    ins = nc.tensor.matmul(outs[c], hT[0:M_LAST, 0, K_LAST:KM * P], weights(1, KM - 1, M_LAST)[c],
                                           start=False, stop=True)
                ins.then_inc(down_done, 1)

            def entry_of(n):
                entry = pe.value_load(tile_tab[0:1, ds(n, 1)], min_val=1, max_val=4 * BUF_UNIT - 1)
                return entry & (BUF_UNIT - 1), (entry >> 6) & 1, (entry >> 7) & 1

            def by_buffer(product, n, which):
                if isinstance(which, int):
                    product(n, which)
                    return
                with pe.If(which < 1):
                    product(n, 0)
                with pe.Else():
                    product(n, 1)

            def tile(n, entry=None, first=False, last=False):
                ready, buf, buf_before = entry_of(n) if entry is None else entry
                pe.wait_ge(weights_ready, ready)
                pe.wait_ge(xt_high, n + 1)
                pe.wait_ge(xt_low, n + 1)
                if not first:
                    pe.wait_ge(hid_done, n)
                by_buffer(gate_up, n, buf)
                if not first:
                    pe.wait_ge(ht_high, n)
                    pe.wait_ge(ht_low, n)
                if not last:
                    tr_x(n + 1)
                if not first:
                    pe.wait_ge(d_free, n)
                    by_buffer(down, n - 1, buf_before)
                if not last:
                    pe.wait_ge(xt_high, n + 2)
                    pe.wait_ge(xt_low, n + 2)
                tr_h(n)

            def drain_tile(n, buf):
                pe.wait_ge(ht_high, n + 1)
                pe.wait_ge(ht_low, n + 1)
                pe.wait_ge(d_free, n + 1)
                by_buffer(down, n, buf)

            pe.wait_ge(tr_free, B * SETS + 1)
            tr_x(0)
            tile(0, (1, 0, None), first=True)
            with pe.Fori(1, N_ALL) as n:
                tile(n)
            n_tiles = pe.value_load(count_tab[0:1, 0:1], min_val=N_ALL, max_val=N_MAX)
            with pe.Fori(N_ALL, N_MAX) as n:
                with pe.If(n < n_tiles):
                    tile(n)

            tile(n_tiles, (E + 2, 1, entry_of(n_tiles)[2]))
            with pe.Fori(1, TT - 1) as i:
                tile(n_tiles + i, (E + 2, 1, 1))
            tile(n_tiles + (TT - 1), (E + 2, 1, 1), last=True)
            drain_tile(n_tiles + (TT - 1), 1)

        @block.scalar
        def _(act):
            a = nc.scalar
            act.sem_inc(tr_free, 1)
            act.sem_inc(d_free, 1)
            act.sem_inc(d_out, 16)
            act.sem_inc(x1_out, 16)
            act.sem_inc(x2_out, 16)

            def take(high, low, t):
                act.wait_ge(tr_done, t + 2)
                a.activation(high, ps_t[:, 0, :].rearrange("p (k n) -> p k n", k=KH), ACT.Copy)
                a.activation(low, ps_t[:, 1, :].rearrange("p (k n) -> p k n", k=KH), ACT.Copy).then_inc(tr_free, 1)

            def take_ctx(b, j):
                cols = [cT[:, h, :, ds(j * P, P)] for h in range(2)]
                take(cols[0], cols[1], b * SETS + j)

            def take_q(b, j):
                take(xqT[:, 0], xqT[:, 1], b * SETS + set_of_x(j))

            def take_x2(b, t):
                take(xT[:, 0], xT[:, 1], b * SETS + t)

            def high_of_nat(n, t, u):
                act.wait_ge(deq_ready, n + 1)
                act.wait_ge(tr_done, t + 1)
                a.activation(nat[:, 0, :], deq[u], ACT.Copy).then_inc(nat_high, 1)

            def root_q(i, u):
                act.wait_ge(var_q_ready, i + 1)
                a.activation(std_q[:, u:u + 1], var_q[:, u:u + 1], ACT.Sqrt).then_inc(std_q_ready, 1)

            def normalise_q(i, u):
                act.wait_ge(scale_q_ready, i + 1)
                a.activation(qin[u], qin[u], ACT.Identity, scale=scale_q[:, u:u + 1],
                             bias=shift_q[:, u:u + 1]).then_inc(norm_q, 1)

            def root_l(i):
                act.wait_ge(var_l_ready, i + 1)
                a.activation(std_l[:, :], var_l[:, :], ACT.Sqrt).then_inc(std_l_ready, 1)

            def normalise_l(i):
                act.wait_ge(scale_l_ready, i + 1)
                a.activation(x2f, x1b, ACT.Identity, scale=scale_l[:, :], bias=shift_l[:, :]).then_inc(norm_l, 1)

            def high_of_x2(i):
                act.wait_ge(norm_l, i + 1)
                act.wait_ge(x2_out, i * 16 + 16)
                a.activation(x2nat[:, 0, :], x2f, ACT.Copy).then_inc(x2_high, 1)

            def x_tile(b, j, u):
                if not isinstance(j, int) or j < BT - 1:
                    take_q(b, j + 1)
                if not isinstance(j, int) or j < BT - 2:
                    high_of_nat(b * (2 * BT) + j + (BT + 2), b * SETS + set_of_x(j + 1) + 1, u)
                if not isinstance(j, int) or j >= 0:
                    root_l(b * BT + j)
                if not isinstance(j, int) or j < BT - LEAD:
                    root_q(b * BT + j + LEAD, 1 - u)
                if not isinstance(j, int) or j >= 0:
                    normalise_l(b * BT + j)
                if not isinstance(j, int) or j < BT - LEAD:
                    normalise_q(b * BT + j + LEAD, 1 - u)
                if not isinstance(j, int) or j >= 0:
                    high_of_x2(b * BT + j)
                    take_x2(b, SETS - 1 if isinstance(j, int) and j == BT - 1 else set_of_x2(j))

            with act.Fori(0, B) as b:
                i0, n0 = b * BT, b * (2 * BT)
                high_of_nat(n0, b * SETS, 0)
                with act.Fori(0, BT // 2 - 1) as q:
                    for u in range(2):
                        high_of_nat(n0 + q * 2 + (u + 1), b * SETS + q * 2 + (u + 1), 1 - u)
                        take_ctx(b, q * 2 + u)
                high_of_nat(n0 + (BT - 1), b * SETS + (BT - 1), 1)
                take_ctx(b, BT - 2)
                root_q(i0, 0)
                root_q(i0 + 1, 1)
                normalise_q(i0, 0)
                normalise_q(i0 + 1, 1)
                take_ctx(b, BT - 1)
                high_of_nat(n0 + BT, b * SETS + BT, 0)
                x_tile(b, -1, 1)
                x_tile(b, 0, 0)
                with act.Fori(0, (BT - LEAD - 1) // 2) as q:
                    for u in range(2):
                        x_tile(b, q * 2 + (u + 1), 1 - u)
                for j in range(BT - LEAD, BT):
                    x_tile(b, j, j % 2)

            act.wait_ge(top_ready, 1)
            a.activation(top_w[:, :, :], top_w[:, :, :], ACT.Sigmoid, scale=1.0 / WSCALE).then_inc(sig_ready, 1)

            def load_x(n, row):
                act.dma_start(xin[:, :, :].rearrange("p a d -> p (a d)"), rows_x[ds(row, P), :]).then_inc(xin_in, 16)

            def take_xt(n):
                act.wait_ge(trx, n + 1)
                a.activation(xT[:, 0, :, :], ps_t[:, 0, :].rearrange("p (k n) -> p k n", k=KH), ACT.Copy)\
                    .then_inc(xt_high, 1)

            def silu(n):
                act.wait_ge(gu_done, n + 1)
                a.activation(sil[:, :, :], ps_gu[:, 0:2, 0:CH], ACT.Silu, scale=1.0 / WSCALE).then_inc(silu_done, 1)

            def high_of_hidden(n):
                act.wait_ge(hid_done, n + 1)
                a.activation(hid_hl[:, 0:M], hid[:, :, :].rearrange("p a c -> p (a c)"), ACT.Copy)\
                    .then_inc(hid_high, 1)

            def take_ht(n):
                act.wait_ge(trh, n + 1)
                a.activation(hT[:, 0, 0:KM * P], ps_t[:, 0, 0:KM * P], ACT.Copy).then_inc(ht_high, 1)

            def store_d(n):
                act.wait_ge(down_done, n + 1)
                act.wait_ge(d_out, n * 16 + 16)
                a.activation(dout[:, :], ps_d_flat, ACT.Copy, scale=1.0 / (WSCALE * HSCALE)).then_inc(d_free, 1)
                act.wait_ge(d_free, n + 2)
                act.dma_start(rows_d[ds(n * P, P), :], dout[:, :]).then_inc(d_out, 16)

            def tile(n, next_row=None, last=False, store=False):
                silu(n)
                if not last:
                    take_xt(n + 1)
                if next_row is not None:
                    load_x(n + 2, next_row)
                high_of_hidden(n)
                if store:
                    store_d(n - 1)
                take_ht(n)

            act.wait_ge(x2_out, 16 * TT + 16)
            act.wait_ge(routed, 1)
            load_x(0, 0)
            take_xt(0)
            load_x(1, P)
            tile(0, 2 * P)
            with act.Fori(1, A_LAST) as n:
                tile(n, (n + 2) * P, store=True)
            act.wait_ge(pad_out, 16 * E)
            for u in range(2):
                act.wait_ge(scat_out[u], 16 * TOPK * TT // 2)
            with act.Fori(A_LAST, N_ALL - 2) as n:
                tile(n, (n + 2) * P, store=True)
            n_tiles = act.value_load(count_tab[0:1, 0:1], min_val=N_ALL, max_val=N_MAX)
            act.wait_ge(zeros_out, 16)
            with act.Fori(N_ALL - 2, N_MAX) as n:
                with act.If(n < n_tiles):
                    row = act.value_load(row_tab[0:1, ds(n - (N_ALL - 2), 1)], min_val=0, max_val=N_MAX - 1)
                    tile(n, row * P, store=True)

            tile(n_tiles, 2 * P, store=True)
            with act.Fori(1, TT - 2) as i:
                tile(n_tiles + i, (i + 2) * P)
            tile(n_tiles + (TT - 2))
            tile(n_tiles + (TT - 1), last=True)

        @block.vector
        def _(dve):
            v = nc.vector
            dve.sem_inc(qin_free, 2)
            for free in (x1_free, logits_free):
                dve.sem_inc(free, 1)

            def blocks(ap):
                return ap.rearrange("p (k n) -> p k n", k=KH)

            def per_block(ap):
                return ap.unsqueeze(2).to_broadcast([P, KH, P])

            step = Chain(dve, gw_step, 0)
            dve.wait_ge(gw_in, 16)
            step(v.tensor_scalar(gw_f[:, :], gw_f[:, :], WSCALE, None, ALU.mult))
            step(v.tensor_copy(gw[:, 0, :], gw_f[:, :]))
            v.tensor_tensor(gw[:, 1, :], gw_f[:, :], gw[:, 0, :], ALU.subtract).then_inc(gw_ready, 1)
            dve.wait_ge(const_ready, CONSTS)

            def guard(step, block_amax, eps, scale):
                step(v.tensor_scalar(safe[:, :], block_amax, eps, None, ALU.max))
                v.tensor_scalar(from_q[:, :], safe[:, :], 1.0 / FP8_MAX, scale, ALU.mult, ALU.mult)
                step(v.reciprocal(to_q[:, :], safe[:, :]))
                step(v.tensor_scalar(to_q[:, :], to_q[:, :], FP8_MAX, None, ALU.mult))

            def quantise(step, n, u):
                dve.wait_ge(nat_ready, n + 1)
                v.tensor_tensor(blocks(deq[u]), blocks(qin[u]), per_block(to_q[:, :]), ALU.mult)\
                    .then_inc(qin_free, 1)
                dve.wait_ge(qin_free, n + 3)
                step(v.tensor_scalar(rnd.bitcast(I32), deq[u].bitcast(I32), EXP_MASK, None, ALU.bitwise_and))
                step(v.tensor_scalar(rnd, rnd, FP8_MIN_EXP, FP8_ROUND, ALU.max, ALU.mult))
                step(v.tensor_tensor(deq[u], deq[u], rnd, ALU.add))
                step(v.tensor_tensor(deq[u], deq[u], rnd, ALU.subtract))
                v.tensor_tensor(blocks(deq[u]), blocks(deq[u]), per_block(from_q[:, :]), ALU.mult)\
                    .then_inc(deq_ready, 1)

            def ctx_max(c, load, u):
                dve.wait_ge(qin_in[u], load * 16 + 16)
                v.tensor_reduce(amax_p[:, u, :], blocks(qin[u]), AX.X, ALU.max, apply_absolute_value=True)\
                    .then_inc(block_max, 1)

            def ctx_tile(c, n, u):
                step = Chain(dve, ctx_step, c * CTX_STEPS)
                dve.wait_ge(block_max_all, c + 1)
                guard(step, amax[:, u, :], W_EPS, WSCALE)
                quantise(step, n, u)
                assert step.n == CTX_STEPS

            def moments(step, src, stats, mv, var, ready):
                v.bn_stats(stats[:, 0:6], src[:, 0:512])
                step(v.bn_stats(stats[:, 6:12], src[:, 512:1024]))
                dve.sem_inc(dve_turn, 1)
                step(v.bn_aggr(mv, stats[:, :]))
                v.tensor_scalar(var, mv[:, 1:2], LN_EPS, None, ALU.add).then_inc(ready, 1)

            def x_moments(i, load, u):
                dve.wait_ge(qin_in[u], load * 16 + 16)
                moments(Chain(dve, mean_step, i * MEAN_STEPS), qin[u], stats_q, mv_q[:, 2 * u:2 * u + 2],
                        var_q[:, u:u + 1], var_q_ready)

            def x_scale(i, u):
                dve.wait_ge(std_q_ready, i + 1)
                v.reciprocal(scale_q[:, u:u + 1], std_q[:, u:u + 1]).then_inc(scale_step, 1)
                dve.wait_ge(scale_step, i + 1)
                v.tensor_scalar(shift_q[:, u:u + 1], mv_q[:, 2 * u:2 * u + 1], scale_q[:, u:u + 1], -1.0,
                                ALU.mult, ALU.mult).then_inc(scale_q_ready, 1)

            def x_tile(i, n, u):
                step = Chain(dve, x_step, i * X_STEPS)
                dve.wait_ge(norm_q, i + 1)
                step(v.tensor_reduce(amax[:, u, :], blocks(qin[u]), AX.X, ALU.max, apply_absolute_value=True))
                guard(step, amax[:, u, :], ACT_EPS, 1.0)
                quantise(step, n, u)
                assert step.n == X_STEPS

            def residual(i):
                step = Chain(dve, ln_step, i * LN_STEPS)
                dve.wait_ge(attn_done, i + 1)
                dve.wait_ge(xres_in, i * 16 + 16)
                dve.wait_ge(x1_out, i * 16 + 16)
                v.scalar_tensor_tensor(out=x1b, in0=ps_d_flat, scalar=1.0 / WSCALE, in1=xres, op0=ALU.mult,
                                       op1=ALU.add).then_inc(x1_free, 1)
                dve.wait_ge(x1_free, i + 2)
                moments(step, x1b, stats_l, mv_l[:, :], var_l[:, :], var_l_ready)

            def x2_scale(i):
                step = Chain(dve, ln_step, i * LN_STEPS + (LN_STEPS - 1))
                dve.wait_ge(std_l_ready, i + 1)
                step(v.reciprocal(scale_l[:, :], std_l[:, :]))
                v.tensor_scalar(shift_l[:, :], mv_l[:, 0:1], scale_l[:, :], -1.0, ALU.mult,
                                ALU.mult).then_inc(scale_l_ready, 1)

            def choose(i):
                step = Chain(dve, top_step, i * TOP_STEPS)
                dve.wait_ge(logits_done, i + 1)
                step(v.tensor_reduce(group8[:, 0:GROUPS], ps_logits.rearrange("p (g e) -> p g e", g=GROUPS), AX.X,
                                     ALU.max))
                dve.sem_inc(dve_turn, 1)
                step(v.max(group_top[:, :], group8[:, :]))
                dve.sem_inc(dve_turn, 1)
                step(v.max_index(group_idx[:, :], group_top[:, :], group8[:, :]))
                step(v.tensor_copy(group_f[:, :], group_idx[:, 0:TOPG]))
                step(v.tensor_scalar(chosen[:, :], iota_e[:, 0:GROUPS], group_f[:, 0:1], None, ALU.is_equal))
                step(v.scalar_tensor_tensor(out=chosen2[:, :], in0=iota_e[:, 0:GROUPS], scalar=group_f[:, 1:2],
                                            in1=chosen[:, :], op0=ALU.is_equal, op1=ALU.add))
                step(v.tensor_scalar(chosen[:, :], chosen2[:, :], -NEG, NEG, ALU.mult, ALU.add))
                v.tensor_tensor(masked[:, :].rearrange("p (g e) -> p g e", g=GROUPS),
                                ps_logits.rearrange("p (g e) -> p g e", g=GROUPS),
                                chosen[:, :].unsqueeze(2).to_broadcast([P, GROUPS, E // GROUPS]),
                                ALU.add).then_inc(logits_free, 1)
                dve.wait_ge(logits_free, i + 2)
                dve.sem_inc(dve_turn, 1)
                step(v.max(expert_top[:, :], masked[:, :]))
                dve.sem_inc(dve_turn, 1)
                step(v.max_index(expert_idx[:, :], expert_top[:, :], masked[:, :]))
                v.tensor_copy(top_w[:, ds(i, 1), :].rearrange("p a k -> p (a k)"), expert_top[:, 0:TOPK])
                step(v.tensor_copy(top_idx[:, ds(i, 1), :].rearrange("p a k -> p (a k)"), expert_idx[:, 0:TOPK]))
                assert step.n == TOP_STEPS

            def x_step_of(b, j, u, half):
                i, n = b * BT + j, b * (2 * BT) + j + BT
                ahead = not isinstance(j, int) or j < BT - LEAD
                residual(i)
                if ahead:
                    x_moments(i + LEAD, b * BT + half + BT // 2, 1 - u)
                x2_scale(i)
                if ahead:
                    x_scale(i + LEAD, 1 - u)
                if not isinstance(j, int) or j > 0:
                    choose(i - 1)
                if ahead:
                    x_tile(i + LEAD, n + LEAD, 1 - u)

            with dve.Fori(0, B) as b:
                i0, n0 = b * BT, b * (2 * BT)
                ctx_max(i0, i0, 0)
                with dve.Fori(0, BT // 2 - 1) as q:
                    for u in range(2):
                        ctx_max(i0 + q * 2 + (u + 1), i0 + q + u, 1 - u)
                        ctx_tile(i0 + q * 2 + u, n0 + q * 2 + u, u)
                ctx_max(i0 + (BT - 1), i0 + (BT // 2 - 1), 1)
                ctx_tile(i0 + (BT - 2), n0 + (BT - 2), 0)
                ctx_tile(i0 + (BT - 1), n0 + (BT - 1), 1)
                x_moments(i0, i0 + BT // 2, 0)
                x_moments(i0 + 1, i0 + BT // 2, 1)
                x_scale(i0, 0)
                x_scale(i0 + 1, 1)
                x_tile(i0, n0 + BT, 0)
                x_tile(i0 + 1, n0 + (BT + 1), 1)
                x_moments(i0 + 2, i0 + (BT // 2 + 1), 0)
                x_scale(i0 + 2, 0)
                x_tile(i0 + 2, n0 + (BT + 2), 0)
                x_step_of(b, 0, 0, LEAD // 2)
                with dve.Fori(0, (BT - LEAD - 1) // 2) as q:
                    for u in range(2):
                        x_step_of(b, q * 2 + (u + 1), 1 - u, q + (1 + LEAD) // 2)
                for j in range(BT - LEAD, BT):
                    x_step_of(b, j, j % 2, None)
                choose(i0 + (BT - 1))

            dve.sem_inc(top_ready, 1)
            dve.wait_ge(x1_out, 16 * TT + 16)
            dve.wait_ge(x2_out, 16 * TT + 16)
            step = Chain(dve, route_step, 0)
            full = [P, TT, TOPK, E]
            for k in range(TOPK):
                last = v.tensor_tensor(hot[:, :, k, :], top_idx[:, :, k:k + 1].to_broadcast([P, TT, E]),
                                       iota_e[:, :].unsqueeze(1).to_broadcast([P, TT, E]), ALU.is_equal)
            step(last)
            with nc.allow_low_precision(reason="at most one of the six is 1"):
                step(v.tensor_reduce(mask, hot.rearrange("p t k e -> p t e k"), AX.X, ALU.add))
            v.memset(pre_a[:, 0:1, :], 0.0)
            step(v.tensor_copy(pre_a[:, 1:TT, :], mask[:, 0:TT - 1, :]))
            src, dst, d = pre_a, pre_b, 1
            while d < TT:
                v.tensor_copy(dst[:, 0:d, :], src[:, 0:d, :])
                step(v.tensor_tensor(dst[:, d:TT, :], src[:, d:TT, :], src[:, 0:TT - d, :], ALU.add))
                src, dst, d = dst, src, 2 * d
            assert src is pre_b
            dve.sem_inc(mask_ready, 1)
            dve.wait_ge(sig_ready, 1)
            step(v.tensor_reduce(w_sum[:, :], top_w[:, :, :], AX.X, ALU.add))
            step(v.reciprocal(w_sum[:, :], w_sum[:, :]))
            step(v.tensor_tensor(top_w[:, :, :], top_w[:, :, :],
                                 w_sum[:, :].unsqueeze(2).to_broadcast([P, TT, TOPK]), ALU.mult))
            dve.wait_ge(rank_done, 1)
            step(v.tensor_copy(count[:, :], ps_gu[:, 2, 0:E]))
            step(v.tensor_scalar(tiles_e[:, :], count[:, :], P - 1.0, 1.0 / P, ALU.add, ALU.mult))
            step(v.tensor_scalar(tiles_e[:, :], tiles_e[:, :], -127.0 / 256, 2.0 ** 23, ALU.add, ALU.add))
            step(v.tensor_scalar(tiles_e[:, :], tiles_e[:, :], -2.0 ** 23, None, ALU.add))
            step(v.tensor_tensor_scan(ends[:, :], ones_f[:, :], tiles_e[:, :], 0.0, ALU.mult, ALU.add))
            step(v.tensor_tensor(first_slot[:, :], ends[:, :], tiles_e[:, :], ALU.subtract))
            step(v.tensor_scalar(first_slot[:, :], first_slot[:, :], float(P), float(T), ALU.mult, ALU.add))
            step(v.tensor_tensor(place, ps_gu[:, 0:2, :].rearrange("p a (t e) -> p (a t) e", e=E),
                                 first_slot[:, :].unsqueeze(1).to_broadcast([P, TT, E]), ALU.add))
            for k in range(TOPK):
                last = v.tensor_tensor(prod[:, :, k, :], hot[:, :, k, :], place, ALU.mult)
            step(last)
            step(v.tensor_reduce(top_idx[:, :, :], prod, AX.X, ALU.add))
            step(v.tensor_copy(slot[:, :, :], top_idx[:, :, :]))
            step(v.tensor_tensor(tab_cmp, iota_t[0:1, :].unsqueeze(2).to_broadcast([1, SLOT_TILES, E]),
                                 ends[0:1, :].unsqueeze(1).to_broadcast([1, SLOT_TILES, E]), ALU.is_ge))
            step(v.tensor_reduce(expert_t[0:1, :], tab_cmp, AX.X, ALU.add))
            v.memset(ready_tab[0:1, 0:TT], 1)
            v.memset(buf_tab[0:1, 0:TT], 0)
            v.memset(tile_tab[0:1, 0:TT], 1)
            v.memset(tile_tab[0:1, N_MAX:], 0)
            v.tensor_scalar(count_f[0:1, :], ends[0:1, E - 1:E], float(TT), None, ALU.add)
            v.memset(done_tab[0:1, 0:1], 1)
            v.memset(done_tab[0:1, 1:2], TT)
            v.tensor_scalar(done_tab[0:1, 2:E + 2], ends[0:1, :], float(TT), None, ALU.add)
            v.tensor_scalar(count_tab[0:1, :], ends[0:1, E - 1:E], float(TT), None, ALU.add)
            step(v.tensor_scalar(ready_tab[0:1, TT:], expert_t[0:1, :], E - 1.0, 2.0, ALU.min, ALU.add))
            step(v.tensor_scalar(buf_tab[0:1, TT:], ready_tab[0:1, TT:], 1, 1, ALU.bitwise_and, ALU.bitwise_xor))
            step(v.scalar_tensor_tensor(out=tile_tab[0:1, TT:N_MAX], in0=buf_tab[0:1, TT:], scalar=BUF_UNIT,
                                        in1=ready_tab[0:1, TT:], op0=ALU.mult, op1=ALU.add))
            step(v.scalar_tensor_tensor(out=tile_tab[0:1, TT:], in0=buf_tab[0:1, TT - 1:],
                                        scalar=2 * BUF_UNIT, in1=tile_tab[0:1, TT:], op0=ALU.mult, op1=ALU.add))
            step(v.tensor_scalar(row_wrap[:, :], row_n[:, :], ends[0:1, E - 1:E], float(TT), ALU.subtract,
                                 ALU.subtract))
            step(v.tensor_scalar(row_wrap[:, :], row_wrap[:, :], 0.0, None, ALU.is_ge))
            step(v.tensor_scalar(row_wrap[:, :], row_wrap[:, :], count_f[0:1, :], None, ALU.mult))
            step(v.tensor_tensor(row_tab[:, :], row_n[:, :], row_wrap[:, :], ALU.subtract))
            step(v.tensor_scalar(tmp_e[:, :], tiles_e[:, :], float(P), iota_p[:, :], ALU.mult, ALU.add))
            step(v.scalar_tensor_tensor(out=tmp_e[:, :], in0=tmp_e[:, :], scalar=-float(P), in1=count[:, :],
                                        op0=ALU.add, op1=ALU.is_ge))
            step(v.tensor_scalar(first_slot[:, :], ends[:, :], float(P), iota_p[:, :], ALU.mult, ALU.add))
            step(v.tensor_scalar(first_slot[:, :], first_slot[:, :], T - P + FAR, None, ALU.add))
            v.scalar_tensor_tensor(out=pad_idx[:, :], in0=tmp_e[:, :], scalar=-FAR, in1=first_slot[:, :],
                                   op0=ALU.mult, op1=ALU.add).then_inc(routed, 1)

            def take_xt(n):
                dve.wait_ge(trx, n + 1)
                v.tensor_copy(xT[:, 1, :, :].rearrange("p k n -> p (k n)"), ps_t[:, 1, :]).then_inc(xt_low, 1)

            def hidden(n):
                dve.wait_ge(silu_done, n + 1)
                v.scalar_tensor_tensor(out=hid[:, :, :], in0=ps_gu[:, 2:4, 0:CH], scalar=HSCALE / WSCALE,
                                       in1=sil[:, :, :], op0=ALU.mult, op1=ALU.mult).then_inc(hid_done, 1)

            def low_of_hidden(n):
                dve.wait_ge(hid_high, n + 1)
                flat = hid[:, :, :].rearrange("p a c -> p (a c)")
                v.tensor_tensor(hid_hl[:, M:M + M_LAST], flat[:, K_LAST:], hid_hl[:, K_LAST:M], ALU.subtract)
                v.tensor_tensor(hid_hl[:, M + M_LAST:], flat[:, 0:K_LAST], hid_hl[:, 0:K_LAST],
                                ALU.subtract).then_inc(hid_low, 1)

            def take_ht(n):
                dve.wait_ge(trh, n + 1)
                v.tensor_copy(hT[:, 1, 0:K_LAST], ps_t[:, 1, 0:K_LAST]).then_inc(ht_low, 1)

            def tile(n, last=False, before=None):
                hidden(n)
                if not last:
                    take_xt(n + 1)
                low_of_hidden(n)
                if before is not None:
                    combine(*before)
                take_ht(n)

            def combine(i, u, pair):
                step = Chain(dve, comb_step, i * COMB_STEPS)
                dve.wait_ge(down_done, n_tiles + (i + 1))
                dve.wait_ge(side_in[u], pair * 32 + 32)
                v.scalar_tensor_tensor(out=total[u], in0=ps_d_flat, scalar=1.0 / (WSCALE * HSCALE), in1=total[u],
                                       op0=ALU.mult, op1=ALU.add).then_inc(d_free, 1)
                dve.wait_ge(d_free, n_tiles + (i + 2))
                step(v.tensor_tensor(total[u], total[u], a_rows[u], ALU.add))
                dve.wait_ge(gat_in[u], pair * (16 * TOPK) + 16 * TOPK)
                for k in range(TOPK):
                    ins = v.scalar_tensor_tensor(
                        out=total[u], in0=gat[u][:, k, :],
                        scalar=top_w[:, ds(i, 1), k:k + 1].rearrange("p a k -> p (a k)"), in1=total[u],
                        op0=ALU.mult, op1=ALU.add)
                    if k < TOPK - 1:
                        step(ins)
                    else:
                        ins.then_inc(comb_done, 1)
                assert step.n == COMB_STEPS

            take_xt(0)
            with dve.Fori(0, N_ALL) as n:
                tile(n)
            n_tiles = dve.value_load(count_tab[0:1, 0:1], min_val=N_ALL, max_val=N_MAX)
            with dve.Fori(N_ALL, N_MAX) as n:
                with dve.If(n < n_tiles):
                    tile(n)

            tile(n_tiles)
            with dve.Fori(0, TT // 2 - 1) as q:
                tile(n_tiles + (q * 2 + 1), before=(q * 2, 0, q))
                tile(n_tiles + (q * 2 + 2), before=(q * 2 + 1, 1, q))
            tile(n_tiles + (TT - 1), last=True, before=(TT - 2, 0, TT // 2 - 1))
            combine(TT - 1, 1, TT // 2 - 1)


_INS = ["x", "ctx_2048", "L0_ffn_gate_w", "L0_ffn_w_gate", "L0_ffn_w_up", "L0_ffn_w_down", "L0_ffn_sw_gate",
        "L0_ffn_sw_up", "L0_ffn_sw_down"]


def kernel(**inputs):
    import numpy as _np
    import concourse.bacc as _bacc
    from concourse.bass_utils import run_bass_kernel_spmd as _run

    nc = _bacc.Bacc("TRN2", target_bir_lowering=False, num_devices=1)
    arrays, args = {}, []
    for name in _INS:
        a = _np.ascontiguousarray(inputs[name])
        arrays[f"in_{name}"] = a
        args.append(nc.dram_tensor(f"in_{name}", a.shape, mybir.dt.from_np(a.dtype), kind="ExternalInput").ap())
    out = nc.dram_tensor("out_0", (B, S, H), F32, kind="ExternalOutput").ap()
    build(nc, *args, out)
    r = _run(nc, [arrays], core_ids=[0])
    return r.results[0]["out_0"]
```
